# Optimizing a Trainium2 kernel written in Bass

```python
import numpy as np
import jax
import jax.numpy as jnp

def _softmax(x, axis=-1):
    return jax.nn.softmax(x, axis=axis)

def _gelu(x):
    return jax.nn.gelu(x, approximate=True)

def _silu(x):
    return jax.nn.silu(x)

def _sigmoid(x):
    return jax.nn.sigmoid(x)

def _layernorm(x, axis=-1, eps=1e-05):
    m = jnp.mean(x, axis=axis, keepdims=True)
    v = jnp.var(x, axis=axis, keepdims=True)
    return (x - m) / jnp.sqrt(v + eps)

def _scatter_add(tgt, idx, src, axis=0):
    return tgt.at[idx].add(src)

def _segment_sum(src, seg, n):
    return jax.ops.segment_sum(src, seg, n)
kernel_name = 'mk_gnn_resnorm_d1_gnn_r8_8e77fd'

def setup_inputs(seed: int=0):
    np.random.seed(seed)
    _w = jnp.asarray

    def _rec_inputs():
        import jax
        import jax.numpy as jnp
        _gk = jax.random.key(seed)
        x = -0.000202 + 1 * jax.random.normal(jax.random.fold_in(_gk, 1), (12500, 128), jnp.float32)
        _s = jax.random.randint(jax.random.fold_in(_gk, 2), (200000,), 0, 12500, jnp.int32)
        _d = jax.random.randint(jax.random.fold_in(_gk, 3), (200000,), 0, 12500, jnp.int32)
        _loop = jnp.arange(12500, dtype=jnp.int32)
        src = jnp.concatenate([_s, _d, _loop])
        dst = jnp.concatenate([_d, _s, _loop])
        _o = jnp.argsort(dst, stable=True)
        src = src[_o]
        dst = dst[_o]
        edge_attr_64 = -5.3897e-05 + 0.999841 * jax.random.normal(jax.random.fold_in(_gk, 11), (412500, 64), jnp.float32)
        return (x, src, dst, edge_attr_64)
    x, src, dst, edge_attr_64 = _rec_inputs()

    def _L0_gnn_setup():
        import jax, jax.numpy as jnp
        import numpy as np
        N, E, D, DE, H = (6250, 50000, 128, 64, 8)
        EPS = 1e-05
        SLOPE = 0.2
        key = jax.random.key(seed)
        ks = jax.random.split(key, 16)

        def lin(k, fan_in, fan_out):
            return (jax.random.normal(k, (fan_in, fan_out), jnp.float32) / np.sqrt(fan_in)).astype(jnp.float32)
        return {'node_features': jax.random.normal(ks[0], (N, D), jnp.float32), 'edge_features': jax.random.normal(ks[1], (E, DE), jnp.float32), 'Wn': lin(ks[2], D, D), 'bn': jnp.zeros((D,), jnp.float32), 'Wq': lin(ks[3], D, D), 'bq': jnp.zeros((D,), jnp.float32), 'Wk': lin(ks[4], D, D), 'bk': jnp.zeros((D,), jnp.float32), 'Wv': lin(ks[5], D, D), 'bv': jnp.zeros((D,), jnp.float32), 'We': lin(ks[6], DE, D), 'be': jnp.zeros((D,), jnp.float32), 'A1': lin(ks[7], 3 * D, D), 'b1': jnp.zeros((D,), jnp.float32), 'A2': lin(ks[8], D, H), 'b2': jnp.zeros((H,), jnp.float32), 'gamma': jnp.ones((D,), jnp.float32), 'beta': jnp.zeros((D,), jnp.float32), 'edge_index': jax.random.randint(ks[9], (2, E), 0, N, dtype=jnp.int32)}
    _L0_gnn_all = _L0_gnn_setup()
    _L0_gnn_in = {k: v for k, v in _L0_gnn_all.items() if k in ('Wn', 'bn', 'Wq', 'bq', 'Wk', 'bk', 'Wv', 'bv', 'We', 'be', 'A1', 'b1', 'A2', 'b2', 'gamma', 'beta')}
    del _L0_gnn_all
    return {'x': x, 'src': src, 'dst': dst, 'edge_attr_64': edge_attr_64, 'L0_gnn_Wn': _L0_gnn_in['Wn'], 'L0_gnn_bn': _L0_gnn_in['bn'], 'L0_gnn_Wq': _L0_gnn_in['Wq'], 'L0_gnn_bq': _L0_gnn_in['bq'], 'L0_gnn_Wk': _L0_gnn_in['Wk'], 'L0_gnn_bk': _L0_gnn_in['bk'], 'L0_gnn_Wv': _L0_gnn_in['Wv'], 'L0_gnn_bv': _L0_gnn_in['bv'], 'L0_gnn_We': _L0_gnn_in['We'], 'L0_gnn_be': _L0_gnn_in['be'], 'L0_gnn_A1': _L0_gnn_in['A1'], 'L0_gnn_b1': _L0_gnn_in['b1'], 'L0_gnn_A2': _L0_gnn_in['A2'], 'L0_gnn_b2': _L0_gnn_in['b2'], 'L0_gnn_gamma': _L0_gnn_in['gamma'], 'L0_gnn_beta': _L0_gnn_in['beta']}

def reference(x, src, dst, edge_attr_64, L0_gnn_Wn, L0_gnn_bn, L0_gnn_Wq, L0_gnn_bq, L0_gnn_Wk, L0_gnn_bk, L0_gnn_Wv, L0_gnn_bv, L0_gnn_We, L0_gnn_be, L0_gnn_A1, L0_gnn_b1, L0_gnn_A2, L0_gnn_b2, L0_gnn_gamma, L0_gnn_beta):
    import jax
    import jax.numpy as jnp

    def _L0_gnn_ref(node_features, edge_features, Wn, bn, Wq, bq, Wk, bk, Wv, bv, We, be, A1, b1, A2, b2, gamma, beta, edge_index):
        import jax, jax.numpy as jnp
        import numpy as np
        N, E, D, DE, H = (6250, 50000, 128, 64, 8)
        EPS = 1e-05
        SLOPE = 0.2
        num_nodes = node_features.shape[0]
        h = node_features @ Wn + bn
        q = node_features @ Wq + bq
        k = node_features @ Wk + bk
        v = node_features @ Wv + bv
        eh = edge_features @ We + be
        src, tgt = (edge_index[0], edge_index[1])
        attn_in = jnp.concatenate([q[src], k[tgt], eh], axis=-1)
        hmid = jax.nn.leaky_relu(attn_in @ A1 + b1, SLOPE)
        scores = jax.nn.leaky_relu(hmid @ A2 + b2, SLOPE)
        w = jax.nn.softmax(scores.mean(axis=-1), axis=0)
        out = jax.ops.segment_sum(w[:, None] * v[tgt], src, num_segments=num_nodes)
        y = h + out
        mu = y.mean(axis=-1, keepdims=True)
        var = y.var(axis=-1, keepdims=True)
        return gamma * (y - mu) / jnp.sqrt(var + EPS) + beta
    edge_index = jnp.stack([src, dst])
    x = _layernorm(x + _L0_gnn_ref(x, edge_attr_64, L0_gnn_Wn, L0_gnn_bn, L0_gnn_Wq, L0_gnn_bq, L0_gnn_Wk, L0_gnn_bk, L0_gnn_Wv, L0_gnn_bv, L0_gnn_We, L0_gnn_be, L0_gnn_A1, L0_gnn_b1, L0_gnn_A2, L0_gnn_b2, L0_gnn_gamma, L0_gnn_beta, edge_index), axis=-1)
    return x

_drawn_inputs = setup_inputs


def setup_inputs(seed=0):
    import zlib

    import numpy as np

    out = dict(_drawn_inputs(seed))
    spreads = {'L0_gnn_bn': (0.0, 0.1),
     'L0_gnn_bq': (0.0, 0.8),
     'L0_gnn_bk': (0.0, 0.8),
     'L0_gnn_bv': (0.0, 2.0),
     'L0_gnn_be': (0.0, 0.8),
     'L0_gnn_b1': (0.0, 0.8),
     'L0_gnn_b2': (0.0, 0.8),
     'L0_gnn_gamma': (1.0, 0.2),
     'L0_gnn_beta': (0.0, 0.1)}
    factors = {'edge_attr_64': 55.476,
     'L0_gnn_Wq': 64.0,
     'L0_gnn_Wk': 58.138,
     'L0_gnn_Wv': 64.0,
     'L0_gnn_We': 56.515,
     'L0_gnn_A1': 55.839,
     'L0_gnn_A2': 53.817}
    for name, (base, spread) in spreads.items():
        noise = np.random.default_rng([zlib.crc32(name.encode()), seed]).standard_normal(out[name].shape)
        drawn = base * np.exp(spread * noise) if base else spread * noise
        out[name] = jnp.asarray(drawn.astype(out[name].dtype))
    for name, factor in factors.items():
        out[name] = (out[name] * factor).astype(out[name].dtype)
    return out
```

```python
from contextlib import ExitStack

import numpy as np
import concourse.bass as bass
from concourse import mybir

F32 = mybir.dt.float32
BF16 = mybir.dt.bfloat16
I32 = mybir.dt.int32
ALU = mybir.AluOpType
ACT = mybir.ActivationFunctionType
AX_X = mybir.AxisListType.X
RED = bass.bass_isa.ReduceOp

P = 128
GROUP = 512
TILES = GROUP // P
PAIR = 2 * GROUP
PT = PAIR // P
CHUNK = 7
EXTRA = 3
SLOPE = 0.2
EPS = 1e-5
KEY = 8192.0


def largest_divisor(n, most):
    return max(d for d in range(1, most + 1) if n % d == 0)


def roll(eng, total, peel, ring, step):
    for n in range(peel):
        step(n, n % ring, n // ring)
    assert (total - peel) % ring == 0 and total > peel
    with eng.Fori(0, (total - peel) // ring) as i:
        for u in range(ring):
            n = peel + u
            step(n + ring * i, n % ring, n // ring + i)


def wait(eng, sem, value):
    if not isinstance(value, int) or value > 0:
        eng.wait_ge(sem, value)


def build(nc, x_rows, x_aligned, x_strided, edges, src_pairs, dst_pairs, src_tiles, dst_tiles, wqT, wkT, weT, wv, wn,
          bn, bq, bk, bv, be, A1, b1, A2, b2, gamma, beta, out, n_edges):
    n_pad, D = x_rows.shape
    H = A2.shape[1]
    DE = weT.shape[1]
    pairs = edges.shape[0]
    groups = 2 * pairs
    tiles = PT * pairs
    chunks, _, CW = x_aligned.shape
    blocks = chunks * CHUNK
    assert CW == CHUNK * P and blocks * P == n_pad and D == P and 2 * DE == P and tiles < KEY
    info_parts = largest_divisor(groups, P)
    info_cols = groups // info_parts
    key_parts = largest_divisor(tiles, P)
    key_cols = tiles // key_parts

    pq_dram = nc.dram_tensor("pq_dram", (n_pad, D), F32).ap()
    sum_dram = nc.dram_tensor("sum_dram", (n_pad + P, D), F32).ap()
    span_dram = nc.dram_tensor("span_dram", (groups, 2), I32).ap()

    with ExitStack() as ctx:
        def sb(name, shape, dt):
            return ctx.enter_context(nc.sbuf_tensor(name, shape, dt))

        def ps(name, shape, dt):
            return ctx.enter_context(nc.psum_tensor(name, shape, dt))

        def sem(name):
            return ctx.enter_context(nc.semaphore(name))

        pk = sb("pk", [P, blocks + EXTRA, 3, P], BF16)
        xa = sb("xa", [P, 2, CW], F32)
        stage = sb("stage", [P, 2, CW], F32)
        pk_rest = sb("pk_rest", [P, 2, CW], F32)
        pk_mid = sb("pk_mid", [P, 2, CW], BF16)
        w_in = sb("w_in", [P, 2, P], F32)
        we_in = sb("we_in", [P, 2, P], F32)
        a1_in = sb("a1_in", [P, 3, P], F32)
        wv_sb = sb("wv_sb", [P, P], F32)
        wn_sb = sb("wn_sb", [P, P], F32)
        a2_sb = sb("a2_sb", [P, H], F32)
        bcols = sb("bcols", [P, 3], F32)
        b1_row = sb("b1_row", [P, P], F32)
        b2_row = sb("b2_row", [P, H], F32)
        bv_row = sb("bv_row", [P, P], F32)
        bn_row = sb("bn_row", [P, P], F32)
        gamma_row = sb("gamma_row", [P, P], F32)
        beta_row = sb("beta_row", [P, P], F32)
        w_fold = sb("w_fold", [P, 4, P], F32)
        b_rep = sb("b_rep", [P, 3, P], F32)
        bias_row = sb("bias_row", [P, P], F32)
        iota_i = sb("iota_i", [P, P], I32)
        iota_f = sb("iota_f", [P, P], F32)
        row_i = sb("row_i", [P, P], I32)
        ident = sb("ident", [P, P], F32)
        before = sb("before", [P, P], F32)
        ones_f = sb("ones_f", [P, P], F32)
        ones_b = sb("ones_b", [P, 1], BF16)
        spans = sb("spans", [info_parts, 8, info_cols], I32)
        span_row = sb("span_row", [1, groups, 2], I32)
        rounds_f = sb("rounds_f", [1, groups], F32)
        sums_f = sb("sums_f", [1, groups], F32)
        zeros_f = sb("zeros_f", [1, groups], F32)
        info = sb("info", [1, groups, 4], I32)
        edge = sb("edge", [P, 2, GROUP], F32)
        dst_b = sb("dst_b", [P, 2, PAIR], I32)
        src_i = sb("src_i", [P, 2, PT], I32)
        rows = sb("rows", [P, 4, TILES, P], F32)
        onehot = sb("onehot", [P, 2, GROUP], BF16)
        extra = sb("extra", [P, EXTRA, GROUP], BF16)
        sloped = sb("sloped", [P, 2, GROUP], F32)
        hidden = sb("hidden", [P, 2, GROUP], F32)
        head_b = sb("head_b", [P, PT, H], F32)
        head_l = sb("head_l", [P, PT, H], F32)
        score = sb("score", [P, tiles], F32)
        cols = sb("cols", [P, 16], F32)
        nonzero = sb("nonzero", [P, tiles], BF16)
        key = sb("key", [P, key_cols], F32)
        flag = sb("flag", [P, key_cols], F32)
        count_i = sb("count_i", [1, 1], I32)
        tile_i = sb("tile_i", [1, 1], I32)
        seg_row = sb("seg_row", [P, P], I32)
        seg_col = sb("seg_col", [P, 2], I32)
        seg_f = sb("seg_f", [P, 8], F32)
        seg_to = sb("seg_to", [P, 1], I32)
        seg_x = sb("seg_x", [P, P], F32)
        seg_w = sb("seg_w", [P, P], F32)
        seg_s = sb("seg_s", [P, P], F32)
        seg_t = sb("seg_t", [P, P], F32)
        seg_o = sb("seg_o", [P, P], F32)
        pk_words = pk[:, :, :, :].rearrange("p b c n -> p (b c n)").bitcast(F32)
        span_in = pk_words[0:info_parts, 0:info_cols * GROUP].bitcast(I32)
        x_res = pk_words[:, 0:blocks * P]
        stats = sb("stats", [P, 2, CHUNK, 6], F32)
        moments = sb("moments", [P, 2, CHUNK, 2], F32)
        std = sb("std", [P, 2, CHUNK], F32)
        rstd = sb("rstd", [P, 2, CHUNK], F32)
        shift = sb("shift", [P, 2, CHUNK], F32)
        y = sb("y", [P, 2, CW], F32)

        wide = [ps(f"wide{i}", [P, 1024], F32) for i in range(2)]
        pre = [ps(f"pre{i}", [P, GROUP], F32) for i in range(2)]
        heads = [ps(f"heads{i}", [P, 512], F32) for i in range(2)]

        s_weights = sem("weights_loaded")
        s_passed = sem("passed")
        s_const = sem("constants_made")
        s_rep = sem("bias_columns_repeated")
        s_fold = sem("weights_folded")
        s_folded = sem("folded_copied")
        s_iota = sem("iota_made")
        s_cast = sem("constants_cast")
        s_span_in = sem("dst_for_spans_loaded")
        s_span = sem("span_steps")
        s_span_out = sem("spans_stored")
        s_span_row = sem("spans_back")
        s_info = sem("info_steps")
        s_xa = [sem(f"nodes_loaded{i}") for i in range(2)]
        s_pq_mm = sem("pq_products")
        s_pq_stage = sem("pq_staged")
        s_pq_out = [sem(f"pq_stored{i}") for i in range(2)]
        s_xk = [sem(f"nodes_loaded_again{i}") for i in range(2)]
        s_pk_mm = sem("pk_products")
        s_pk_hi = sem("pk_high_made")
        s_pk_rest = sem("pk_rest_made")
        s_pk_mid = sem("pk_mid_made")
        s_pk_lo = sem("pk_low_made")
        s_sum_init = sem("sums_started")
        s_edge = [sem(f"edges_loaded{i}") for i in range(2)]
        s_dst = [sem(f"dst_loaded{i}") for i in range(2)]
        s_src = [sem(f"src_loaded{i}") for i in range(2)]
        s_rows = [sem(f"rows_gathered{i}") for i in range(4)]
        s_onehot = sem("onehot_ready")
        s_extra = sem("extra_onehots_ready")
        s_extra_used = sem("extra_onehots_used")
        s_pre = sem("pre_ready")
        s_sloped = sem("sloped_ready")
        s_hidden = sem("hidden_ready")
        s_heads = sem("heads_ready")
        s_head_b = sem("heads_biased")
        s_head_l = sem("heads_relued")
        s_score = sem("scores_ready")
        s_soft = sem("softmax_steps")
        s_max = sem("maximum_ready")
        s_exp = sem("exponentials_ready")
        s_total = sem("total_ready")
        s_counts = sem("tile_counts_ready")
        s_left = sem("tiles_counted")
        s_seg_key = sem("segment_key_steps")
        s_seg_max = sem("segment_key_reduced")
        s_seg_tile = sem("segment_tile_known")
        s_seg_in = sem("segment_indices_loaded")
        s_seg_x = sem("segment_rows_gathered")
        s_seg = sem("segment_steps")
        s_seg_mm = sem("segment_products")
        s_seg_add = sem("segment_added")
        s_xs = [sem(f"node_columns_loaded{i}") for i in range(2)]
        s_res = sem("residual_loaded")
        s_sum = [sem(f"sums_loaded{i}") for i in range(2)]
        s_h = sem("node_products")
        s_y = sem("y_ready")
        s_stat = sem("stats_steps")
        s_bn = sem("row_stats_ready")
        s_std = sem("std_ready")
        s_norm = sem("normed")
        s_gam = sem("gamma_applied")
        s_z = sem("residual_added")
        s_out = [sem(f"out_stored{i}") for i in range(2)]

        pq_chunks = pq_dram.rearrange("(p c j) d -> c p (j d)", c=chunks, j=CHUNK)
        sum_chunks = sum_dram[0:n_pad, :].rearrange("(p c j) d -> c p (j d)", c=chunks, j=CHUNK)
        out_chunks = out.rearrange("(p c j) d -> c p (j d)", c=chunks, j=CHUNK)
        x_res_dram = x_rows.rearrange("(p b) d -> p (b d)", p=P)
        WEIGHT_DMAS = 17
        MADE = 9

        block = ctx.enter_context(nc.Block())

        @block.sync
        def _(sp):
            A1_parts = A1.rearrange("(c p) n -> p c n", p=P)
            sp.dma_start(w_in[:, 0, :], wqT).then_inc(s_weights, 16)
            sp.dma_start(a1_in[:, :, :], A1_parts).then_inc(s_weights, 16)
            sp.dma_start(xa[:, 0, :], x_strided[0]).then_inc(s_xa[0], 16)
            sp.dma_start(xa[:, 1, :], x_strided[1]).then_inc(s_xa[1], 16)

            def pq_step(c, slot, turn):
                sp.wait_ge(s_pq_mm, c - 1)
                sp.dma_start(xa[:, slot, :], x_strided[bass.ds(c, 1), :, :].rearrange("a p n -> (a p) n")).then_inc(
                    s_xa[slot], 16)
                sp.wait_ge(s_pq_stage, c - 1)
                pq_store(c - 2, slot)

            def pq_store(c, slot):
                sp.dma_start(pq_chunks[bass.ds(c, 1), :, :].rearrange("a p n -> (a p) n"),
                             stage[:, slot, :]).then_inc(s_pq_out[slot], 16)

            for c in range(2, 4):
                pq_step(c, c % 2, c // 2)
            with sp.Fori(0, (chunks - 4) // 2) as i:
                for u in range(2):
                    pq_step(4 + u + 2 * i, u, 2 + i)
            for c in range(2):
                sp.wait_ge(s_pq_mm, chunks - 1 + c)
                sp.dma_start(xa[:, c, :], x_aligned[c]).then_inc(s_xk[c], 16)
            for c in range(chunks - 2, chunks):
                sp.wait_ge(s_pq_stage, c + 1)
                pq_store(c, c % 2)

            def pair_step(q, slot, turn):
                wait(sp, s_pre, 2 * q - 2)
                sp.dma_start(src_i[:, slot, :], src_pairs[bass.ds(q, 1), :, :].rearrange("a p n -> (a p) n")).then_inc(
                    s_src[slot], 16)
                sp.dma_start(edge[:, slot, :], edges[bass.ds(q, 1), :, :].rearrange("a p n -> (a p) n")).then_inc(
                    s_edge[slot], 16)
                sp.dma_start(dst_b[:, slot, :],
                             dst_pairs[bass.ds(q, 1), :].to_broadcast([P, PAIR])).then_inc(s_dst[slot], 16)

            pair_step(0, 0, 0)
            pair_step(1, 1, 0)

            def pk_step(c, slot, turn):
                sp.wait_ge(s_pk_mm, c - 1)
                sp.dma_start(xa[:, slot, :], x_aligned[bass.ds(c, 1), :, :].rearrange("a p n -> (a p) n")).then_inc(
                    s_xk[slot], 16)

            with sp.Fori(0, (chunks - 2) // 2) as i:
                for u in range(2):
                    pk_step(2 + u + 2 * i, u, 1 + i)

            pair_step(2, 0, 1)
            with sp.Fori(0, (pairs - 3) // 2) as i:
                for u in range(2):
                    pair_step(3 + u + 2 * i, (3 + u) % 2, None)

            sp.wait_ge(s_pre, groups)
            sp.dma_start(x_res, x_res_dram).then_inc(s_res, 16)
            for c in range(2):
                sp.dma_start(xa[:, c, :], x_strided[c]).then_inc(s_xs[c], 16)

            sp.wait_ge(s_left, 1)
            left = sp.value_load(count_i[0:1, 0:1], min_val=1, max_val=tiles)
            with sp.Fori(0, left) as i:
                sp.wait_ge(s_seg_tile, i + 1)
                sp.sem_inc(s_passed, 1)
                t = sp.value_load(tile_i[0:1, 0:1], min_val=0, max_val=tiles - 1)
                sp.dma_start(seg_row[:, :], src_tiles[bass.ds(t, 1), :].to_broadcast([P, P])).then_inc(s_seg_in, 16)
                with nc.allow_non_contiguous_dma(reason="one index per partition"):
                    sp.dma_start(seg_col[:, 0:1], src_tiles[bass.ds(t, 1), :].rearrange("a p -> p a")).then_inc(
                        s_seg_in, 16)
                    sp.dma_start(seg_col[:, 1:2], dst_tiles[bass.ds(t, 1), :].rearrange("a p -> p a")).then_inc(
                        s_seg_in, 16)
            sp.wait_ge(s_seg_add, 16 * left)

            def node_load(c, slot):
                sp.dma_start(stage[:, slot, :], sum_chunks[bass.ds(c, 1), :, :].rearrange("a p n -> (a p) n")).then_inc(
                    s_sum[slot], 16)

            def node_store(c, slot):
                sp.dma_start(out_chunks[bass.ds(c, 1), :, :].rearrange("a p n -> (a p) n"),
                             y[:, slot, :]).then_inc(s_out[slot], 16)

            def node_step(c, slot, turn):
                wait(sp, s_y, c - 1)
                if turn is not None:
                    sp.dma_start(xa[:, slot, :], x_strided[bass.ds(c, 1), :, :].rearrange("a p n -> (a p) n")).then_inc(
                        s_xs[slot], 16)
                node_load(c, slot)
                if turn is not None:
                    sp.wait_ge(s_norm, 2 * (c - 2) + 2)
                    node_store(c - 2, slot)

            node_step(0, 0, None)
            node_step(1, 1, None)
            with sp.Fori(0, (chunks - 2) // 2) as i:
                for u in range(2):
                    node_step(2 + u + 2 * i, u, 1 + i)
            for c in range(chunks - 2, chunks):
                sp.wait_ge(s_norm, 2 * c + 2)
                node_store(c, c % 2)
            for slot in range(2):
                sp.wait_ge(s_out[slot], 16 * (chunks // 2))

        @block.gpsimd
        def _(pool):
            pool.iota(iota_i[:, :], [[P, P]], base=0, channel_multiplier=1).then_inc(s_iota, 1)
            pool.iota(row_i[:, :], [[1, P]], base=0, channel_multiplier=0).then_inc(s_iota, 1)
            pool.memset(ones_f[:, :], 1.0).then_inc(s_const, 1)
            pool.memset(ident[:, :], 0.0).then_inc(s_const, 1)
            pool.memset(ones_b[:, :], 1.0).then_inc(s_const, 1)
            pool.memset(zeros_f[:, :], 0.0).then_inc(s_const, 1)
            pool.memset(info[:, :, :], 0).then_inc(s_const, 1)
            pool.wait_ge(s_const, 5)
            pool.affine_select(out=ident[:, :], in_=ident[:, :], compare_op=ALU.not_equal, fill=1.0, base=0,
                               pattern=[[-1, P]], channel_multiplier=1).then_inc(s_const, 1)
            pool.affine_select(out=before[:, :], in_=ones_f[:, :], compare_op=ALU.is_gt, fill=0.0, base=0,
                               pattern=[[-1, P]], channel_multiplier=1).then_inc(s_const, 1)
            pool.memset(key[:, :], 0.0).then_inc(s_const, 1)
            pool.memset(flag[:, :], 0.0).then_inc(s_const, 1)

            for slot in range(2):
                pool.wait_ge(s_pq_out[slot], 16 * (chunks // 2))

            def pair_step(q, slot, turn):
                for h in range(2):
                    if h == 0:
                        pool.wait_ge(s_src[slot], 16 * (turn + 1))
                    wait(pool, s_pre, 2 * q + h - 3)
                    pool.sem_inc(s_passed, 1)
                    for k in range(TILES):
                        pool.indirect_dma_start(
                            rows[:, 2 * slot + h, k, :], None, pq_dram,
                            bass.IndirectOffsetOnAxis(src_i[:, slot, h * TILES + k:h * TILES + k + 1], 0),
                        ).then_inc(s_rows[2 * slot + h], 16)

            roll(pool, pairs, 3, 2, pair_step)

            pool.wait_ge(s_soft, 2)
            pool.partition_all_reduce(cols[:, 1:2], cols[:, 0:1], P, RED.max).then_inc(s_max, 1)
            pool.wait_ge(s_counts, 4)
            pool.partition_all_reduce(cols[:, 7:8], cols[:, 6:7], P, RED.add).then_inc(s_counts, 1)

            pool.wait_ge(s_left, 1)
            pool.wait_ge(s_sum_init, 16)
            left = pool.value_load(count_i[0:1, 0:1], min_val=1, max_val=tiles)
            with pool.Fori(0, left) as i:
                pool.wait_ge(s_seg_key, 2 * i + 3)
                pool.sem_inc(s_passed, 1)
                pool.partition_all_reduce(cols[:, 9:10], cols[:, 8:9], P, RED.max).then_inc(s_seg_max, 1)
                pool.wait_ge(s_seg_in, 48 * i + 48)
                pool.sem_inc(s_passed, 1)
                pool.indirect_dma_start(seg_x[:, :], None, x_rows,
                                        bass.IndirectOffsetOnAxis(seg_col[:, 1:2], 0)).then_inc(s_seg_x, 16)
                pool.wait_ge(s_seg, 10 * i + 10)
                pool.sem_inc(s_passed, 1)
                pool.indirect_dma_start(sum_dram, bass.IndirectOffsetOnAxis(seg_to[:, 0:1], 0), seg_o[:, :], None,
                                        compute_op=ALU.add).then_inc(s_seg_add, 16)
                pool.wait_ge(s_seg_add, 16 * i + 16)

            pool.wait_ge(s_res, 16)
            pool.wait_ge(s_weights, 16 * WEIGHT_DMAS)

            def beta_step(c):
                xr = x_res[:, bass.ds(c * CW, CW)].rearrange("p (j d) -> p j d", j=CHUNK)
                pool.tensor_tensor(xr, xr, beta_row[:, None, :].to_broadcast([P, CHUNK, P]), ALU.add).then_inc(
                    s_gam, 1)

            def gamma_step(c, slot, turn):
                beta_step(c)
                pool.wait_ge(s_norm, 2 * c + 1)
                yv = y[:, slot, :].rearrange("p (j d) -> p j d", j=CHUNK)
                pool.tensor_tensor(yv, yv, gamma_row[:, None, :].to_broadcast([P, CHUNK, P]), ALU.mult).then_inc(
                    s_gam, 1)

            roll(pool, chunks, 2, 2, gamma_step)

        @block.scalar
        def _(act):
            act.dma_start(w_in[:, 1, :], wkT).then_inc(s_weights, 16)
            act.dma_start(we_in[:, 0, 0:DE], weT).then_inc(s_weights, 16)
            act.dma_start(we_in[:, 1, DE:P], weT).then_inc(s_weights, 16)
            act.dma_start(wv_sb[:, :], wv).then_inc(s_weights, 16)
            act.dma_start(wn_sb[:, :], wn).then_inc(s_weights, 16)
            act.dma_start(a2_sb[:, :], A2).then_inc(s_weights, 16)
            for n, b in enumerate((bq, bk, be)):
                act.dma_start(bcols[:, n:n + 1], b.rearrange("(p a) -> p a", a=1)).then_inc(s_weights, 16)
            act.dma_start(span_in, dst_pairs.rearrange("(p a) n -> p (a n)", p=info_parts)
                          if pairs % info_parts == 0 else
                          dst_pairs.rearrange("a n -> (a n)").rearrange("(p m) -> p m", p=info_parts)).then_inc(
                s_span_in, 16)
            for t, b in ((b1_row, b1), (b2_row, b2), (bv_row, bv), (bn_row, bn), (gamma_row, gamma), (beta_row, beta)):
                act.dma_start(t[:, :], b.rearrange("(a n) -> a n", a=1).to_broadcast([P, b.shape[0]])).then_inc(
                    s_weights, 16)

            act.wait_ge(s_span, 7)
            act.dma_start(span_dram.rearrange("(p g) c -> p (g c)", p=info_parts),
                          spans[:, 6:8, :].rearrange("p a b -> p (a b)")).then_inc(s_span_out, 16)
            act.wait_ge(s_span_out, 16)
            act.dma_start(span_row[:, :, :], span_dram.rearrange("(a g) c -> a g c", a=1)).then_inc(s_span_row, 16)

            act.wait_ge(s_span, 2)

            def pk_step(c, slot, turn):
                act.wait_ge(s_pk_mm, c + 1)
                act.copy(pk[:, bass.ds(c * CHUNK, CHUNK), 0, :],
                         wide[slot][:, 0:CW].rearrange("p (j d) -> p j d", j=CHUNK)).then_inc(s_pk_hi, 1)
                act.wait_ge(s_pk_rest, c + 1)
                wait(act, s_pk_lo, c - 1)
                act.copy(pk_mid[:, slot, :], pk_rest[:, slot, :]).then_inc(s_pk_mid, 1)

            roll(act, chunks, 2, 2, pk_step)

            act.wait_ge(s_weights, 16 * WEIGHT_DMAS)
            act.dma_start(sum_dram.rearrange("(p b) d -> p b d", p=P),
                          bn_row[:, None, :].to_broadcast([P, blocks + 1, P])).then_inc(s_sum_init, 16)

            def pair_step(q, slot, turn):
                for h in range(2):
                    act.wait_ge(s_pre, 2 * q + h + 1)
                    wait(act, s_hidden, 2 * q + h - 1)
                    act.mul(sloped[:, h, :], pre[h][:, :], SLOPE).then_inc(s_sloped, 1)

            roll(act, pairs, 3, 2, pair_step)

            act.wait_ge(s_soft, 3)
            act.activation(score[:, :], score[:, :], ACT.Exp, bias=cols[:, 2:3], scale=1.0 / H,
                           accum_out=cols[:, 3:4]).then_inc(s_exp, 1)

            def norm_step(c, slot, turn):
                for n in range(2):
                    act.wait_ge(s_stat, 6 * c + 3 * n + 1)
                    act.activation(std[:, slot, :], moments[:, slot, :, 1], ACT.Sqrt, bias=cols[:, 12:13]).then_inc(
                        s_std, 1)
                    act.wait_ge(s_stat, 6 * c + 3 * n + 3)
                    for j in range(CHUNK):
                        v = y[:, slot, j * P:(j + 1) * P]
                        last = act.activation(v, v, ACT.Identity, bias=shift[:, slot, j:j + 1],
                                              scale=rstd[:, slot, j:j + 1])
                    last.then_inc(s_norm, 1)

            roll(act, chunks, 2, 2, norm_step)

        @block.tensor
        def _(pe):
            pe.wait_ge(s_weights, 16 * WEIGHT_DMAS)
            pe.wait_ge(s_const, 6)
            pe.wait_ge(s_cast, 2)
            fold = wide[0][:, 0:512].rearrange("p (c n) -> p c n", c=4)
            pe.matmul(fold[:, 0, :], w_in[:, 0, :], a1_in[:, 0, :], start=True, stop=True)
            pe.matmul(fold[:, 1, :], w_in[:, 1, :], a1_in[:, 1, :], start=True, stop=True)
            pe.matmul(fold[:, 2, :], we_in[:, 0, :], a1_in[:, 2, :], start=True, stop=True)
            pe.matmul(fold[:, 3, :], we_in[:, 1, :], a1_in[:, 2, :], start=True, stop=True)
            pe.wait_ge(s_rep, 1)
            for n in range(3):
                last = pe.matmul(wide[1][:, 0:P], b_rep[:, n, :], a1_in[:, n, :], start=(n == 0), stop=(n == 2))
            last.then_inc(s_fold, 1)

            pe.wait_ge(s_folded, 2)

            def table(c, slot, turn, which, loaded, done, free_sem, free):
                pe.wait_ge(loaded[slot], 16 * (turn + 1))
                wait(pe, free_sem, free)
                for j in range(CHUNK):
                    last = pe.matmul(wide[slot][:, j * P:(j + 1) * P], xa[:, slot, j * P:(j + 1) * P],
                                     w_fold[:, which, :], start=True, stop=True)
                last.then_inc(done, 1)

            roll(pe, chunks, 2, 2, lambda c, slot, turn: table(c, slot, turn, 0, s_xa, s_pq_mm, s_pq_stage, c - 1))
            pe.wait_ge(s_pq_stage, chunks)
            roll(pe, chunks, 2, 2, lambda c, slot, turn: table(c, slot, turn, 1, s_xk, s_pk_mm, s_pk_rest, c - 1))

            pe.wait_ge(s_pk_lo, chunks)
            pe.wait_ge(s_pk_hi, chunks)
            pe.wait_ge(s_info, 4)
            pe.sem_inc(s_extra_used, 1)
            flat = pk[:, :, :, :].rearrange("p b c n -> p (b c n)")

            def score_mm(h, slot):
                for k in range(TILES):
                    at = (h * TILES + k) * H
                    last = pe.matmul(heads[slot][:, at:at + H], hidden[:, h, k * P:(k + 1) * P], a2_sb[:, :],
                                     start=True, stop=True)
                last.then_inc(s_heads, 1)

            def pair_step(q, slot, turn):
                for h in range(2):
                    g = 2 * q + h
                    first = pe.value_load(info[0:1, bass.ds(g, 1), 0:1].rearrange("a b c -> a (b c)"),
                                          min_val=0, max_val=blocks - 1)
                    n_extra = pe.value_load(info[0:1, bass.ds(g, 1), 1:2].rearrange("a b c -> a (b c)"),
                                            min_val=0, max_val=blocks // EXTRA + 1)
                    n_before = pe.value_load(info[0:1, bass.ds(g, 1), 2:3].rearrange("a b c -> a (b c)"),
                                             min_val=0, max_val=groups * (blocks // EXTRA + 1))
                    if h == 0:
                        pe.wait_ge(s_edge[slot], 16 * (turn + 1))
                    wait(pe, s_hidden, g - 1)
                    pe.matmul(pre[h][:, :], w_fold[:, 2 + h, :], edge[:, slot, :], start=True, stop=False,
                              skip_group_check=True)
                    pe.wait_ge(s_onehot, g + 1)
                    for c in range(3):
                        pe.matmul(pre[h][:, :], flat[:, bass.ds(first * (3 * P) + c * P, P)], onehot[:, h, :],
                                  start=False, stop=False, skip_group_check=True)
                    with pe.If(n_extra > 0):
                        with pe.Fori(0, n_extra) as r:
                            pe.wait_ge(s_extra, n_before + r + 1)
                            done = (first + r * EXTRA).with_bounds(min_val=0, max_val=blocks - 1)
                            for w in range(EXTRA):
                                for c in range(3):
                                    at = done * (3 * P) + (1 + w) * 3 * P + c * P
                                    last = pe.matmul(pre[h][:, :], flat[:, bass.ds(at, P)], extra[:, w, :],
                                                     start=False, stop=False, skip_group_check=True)
                            last.then_inc(s_extra_used, 1)
                    pe.wait_ge(s_rows[2 * slot + h], 64 * (turn + 1))
                    for k in range(TILES):
                        last = pe.matmul(pre[h][:, k * P:(k + 1) * P], rows[:, 2 * slot + h, k, :], ident[:, :],
                                         start=False, stop=True, skip_group_check=True)
                    last.then_inc(s_pre, 1)
                    if h == 1:
                        pe.wait_ge(s_hidden, g)
                        wait(pe, s_head_b, q - 1)
                        score_mm(0, slot)
                    elif not isinstance(q, int) or q > 0:
                        pe.wait_ge(s_hidden, g)
                        score_mm(1, 1 - slot)

            roll(pe, pairs, 3, 2, pair_step)
            pe.wait_ge(s_hidden, groups)
            score_mm(1, (pairs - 1) % 2)

            pe.wait_ge(s_exp, 1)
            pe.matmul(pre[0][:, 0:1], ones_f[:, :], cols[:, 3:4], start=True, stop=True).then_inc(s_total, 1)
            pe.wait_ge(s_soft, 4)
            for c in range(key_cols):
                last = pe.matmul(pre[1][0:key_parts, c:c + 1], nonzero[:, c * key_parts:(c + 1) * key_parts],
                                 ones_b[:, :], start=True, stop=True)
            last.then_inc(s_counts, 1)

            pe.wait_ge(s_left, 1)
            left = pe.value_load(count_i[0:1, 0:1], min_val=1, max_val=tiles)
            with pe.Fori(0, left) as i:
                pe.wait_ge(s_seg_x, 16 * i + 16)
                pe.wait_ge(s_seg, 10 * i + 3)
                pe.matmul(pre[0][:, 0:P], seg_x[:, :], seg_w[:, :], start=True, stop=True).then_inc(s_seg_mm, 1)
                pe.wait_ge(s_seg, 10 * i + 4)
                pe.matmul(pre[0][:, P:2 * P], seg_t[:, :], wv_sb[:, :], start=True, stop=False)
                pe.matmul(pre[0][:, P:2 * P], seg_w[:, :], bv_row[:, :], start=False, stop=True).then_inc(s_seg_mm, 1)

            def node_step(c, slot, turn):
                pe.wait_ge(s_xs[slot], 16 * (turn + 1))
                wait(pe, s_y, c - 1)
                for j in range(CHUNK):
                    last = pe.matmul(wide[slot][:, j * P:(j + 1) * P], xa[:, slot, j * P:(j + 1) * P], wn_sb[:, :],
                                     start=True, stop=True)
                last.then_inc(s_h, 1)

            roll(pe, chunks, 2, 2, node_step)

        @block.vector
        def _(dve):
            dve.memset(we_in[:, 0, DE:P], 0.0).then_inc(s_cast, 1)
            dve.memset(we_in[:, 1, 0:DE], 0.0).then_inc(s_cast, 1)
            dve.wait_ge(s_iota, 2)
            dve.tensor_copy(iota_f[:, :], iota_i[:, :]).then_inc(s_cast, 1)
            dve.memset(cols[:, 12:13], EPS).then_inc(s_cast, 1)
            dve.wait_ge(s_const, MADE)
            dve.wait_ge(s_weights, 16 * WEIGHT_DMAS)
            dve.tensor_copy(b_rep[:, :, :], bcols[:, :, None].to_broadcast([P, 3, P])).then_inc(s_rep, 1)
            dve.wait_ge(s_fold, 1)
            dve.tensor_copy(w_fold[:, :, :], wide[0][:, 0:512].rearrange("p (c n) -> p c n", c=4)).then_inc(
                s_folded, 1)
            dve.tensor_tensor(bias_row[:, :], wide[1][:, 0:P], b1_row[:, :], ALU.add).then_inc(s_folded, 1)

            dve.wait_ge(s_span_in, 16)
            sv = span_in.rearrange("p (g n) -> p g n", g=info_cols)
            dve.tensor_reduce(spans[:, 0, :], sv, AX_X, ALU.min).then_inc(s_span, 1)
            dve.tensor_reduce(spans[:, 1, :], sv, AX_X, ALU.max).then_inc(s_span, 1)
            dve.wait_ge(s_span, 2)
            dve.tensor_scalar(spans[:, 2:4, :], spans[:, 0:2, :], 7, None, ALU.logical_shift_right).then_inc(s_span, 1)
            dve.wait_ge(s_span, 3)
            dve.tensor_tensor(spans[:, 4, :], spans[:, 3, :], spans[:, 2, :], ALU.subtract).then_inc(s_span, 1)
            dve.wait_ge(s_span, 4)
            scale = (1 << 16) // EXTRA + 1
            dve.tensor_scalar(spans[:, 5, :], spans[:, 4, :], float(EXTRA - 1), float(scale), ALU.add,
                              ALU.mult).then_inc(s_span, 1)
            dve.wait_ge(s_span, 5)
            dve.tensor_copy(spans[:, 6:8, :].rearrange("p a b -> p (a b)").rearrange("p (g c) -> p g c", c=2)[:, :, 0],
                            spans[:, 2, :]).then_inc(s_span, 1)
            dve.tensor_scalar(
                spans[:, 6:8, :].rearrange("p a b -> p (a b)").rearrange("p (g c) -> p g c", c=2)[:, :, 1],
                spans[:, 5, :], 16, None, ALU.logical_shift_right).then_inc(s_span, 1)

            dve.wait_ge(s_folded, 2)

            def pq_step(c, slot, turn):
                dve.wait_ge(s_pq_mm, c + 1)
                wait(dve, s_pq_out[slot], 16 * turn)
                dve.tensor_tensor(stage[:, slot, :].rearrange("p (j d) -> p j d", j=CHUNK),
                                  wide[slot][:, 0:CW].rearrange("p (j d) -> p j d", j=CHUNK),
                                  bias_row[:, None, :].to_broadcast([P, CHUNK, P]), ALU.add).then_inc(s_pq_stage, 1)

            roll(dve, chunks, 2, 2, pq_step)

            dve.memset(pk[:, blocks:blocks + EXTRA, :, :], 0.0).then_inc(s_cast, 1)

            def pk_step(c, slot, turn):
                dve.wait_ge(s_pk_hi, c + 1)
                hi = pk[:, bass.ds(c * CHUNK, CHUNK), 0, :]
                rest = pk_rest[:, slot, :].rearrange("p (j d) -> p j d", j=CHUNK)
                dve.tensor_tensor(rest, wide[slot][:, 0:CW].rearrange("p (j d) -> p j d", j=CHUNK), hi,
                                  ALU.subtract).then_inc(s_pk_rest, 1)
                dve.wait_ge(s_pk_mid, c + 1)
                mid = pk_mid[:, slot, :].rearrange("p (j d) -> p j d", j=CHUNK)
                dve.tensor_copy(pk[:, bass.ds(c * CHUNK, CHUNK), 1, :], mid)
                dve.tensor_tensor(pk[:, bass.ds(c * CHUNK, CHUNK), 2, :], rest, mid, ALU.subtract).then_inc(s_pk_lo, 1)

            roll(dve, chunks, 2, 2, pk_step)

            dve.wait_ge(s_span_row, 16)
            dve.tensor_copy(rounds_f[:, :], span_row[:, :, 1]).then_inc(s_info, 1)
            dve.wait_ge(s_info, 1)
            dve.wait_ge(s_const, 5)
            dve.tensor_tensor_scan(sums_f[:, :], rounds_f[:, :], zeros_f[:, :], 0.0, ALU.add, ALU.add).then_inc(
                s_info, 1)
            dve.wait_ge(s_info, 2)
            dve.tensor_copy(info[:, :, 0:2], span_row[:, :, :]).then_inc(s_info, 1)
            dve.tensor_tensor(info[:, :, 2], sums_f[:, :], rounds_f[:, :], ALU.subtract).then_inc(s_info, 1)
            dve.wait_ge(s_info, 4)
            dve.wait_ge(s_weights, 16 * WEIGHT_DMAS)

            def windows(q, slot, turn, h):
                    g = 2 * q + h
                    dst = dst_b[:, slot, h * GROUP:(h + 1) * GROUP]
                    first = dve.value_load(info[0:1, bass.ds(g, 1), 0:1].rearrange("a b c -> a (b c)"),
                                           min_val=0, max_val=blocks - 1)
                    n_extra = dve.value_load(info[0:1, bass.ds(g, 1), 1:2].rearrange("a b c -> a (b c)"),
                                             min_val=0, max_val=blocks // EXTRA + 1)
                    n_before = dve.value_load(info[0:1, bass.ds(g, 1), 2:3].rearrange("a b c -> a (b c)"),
                                              min_val=0, max_val=groups * (blocks // EXTRA + 1))
                    if h == 0:
                        dve.wait_ge(s_dst[slot], 16 * (turn + 1))
                    wait(dve, s_pre, g - 1)
                    dve.tensor_scalar(onehot[:, h, :], dst, iota_f[:, bass.ds(first, 1)], None,
                                      ALU.is_equal).then_inc(s_onehot, 1)
                    with dve.If(n_extra > 0):
                        with dve.Fori(0, n_extra) as r:
                            dve.wait_ge(s_extra_used, n_before + r + 1)
                            done = (first + r * EXTRA).with_bounds(min_val=0, max_val=blocks - 1)
                            for w in range(EXTRA):
                                last = dve.tensor_scalar(extra[:, w, :], dst,
                                                         iota_f[:, bass.ds(done + (1 + w), 1)], None,
                                                         ALU.is_equal)
                            last.then_inc(s_extra, 1)

            def relu(g, h):
                dve.wait_ge(s_sloped, g + 1)
                wait(dve, s_heads, g - 1)
                dve.tensor_tensor(hidden[:, h, :], pre[h][:, :], sloped[:, h, :], ALU.max).then_inc(s_hidden, 1)

            def scores(q, slot):
                dve.wait_ge(s_heads, 2 * q + 2)
                dve.tensor_tensor(head_b[:, :, :], heads[slot][:, 0:PT * H].rearrange("p (t h) -> p t h", h=H),
                                  b2_row[:, None, :].to_broadcast([P, PT, H]), ALU.add).then_inc(s_head_b, 1)
                dve.wait_ge(s_head_b, q + 1)
                dve.scalar_tensor_tensor(out=head_l[:, :, :], in0=head_b[:, :, :], scalar=SLOPE, in1=head_b[:, :, :],
                                         op0=ALU.mult, op1=ALU.max).then_inc(s_head_l, 1)
                dve.wait_ge(s_head_l, q + 1)
                dve.tensor_reduce(score[:, bass.ds(q * PT, PT)], head_l[:, :, :], AX_X, ALU.add).then_inc(s_score, 1)

            def pair_step(q, slot, turn):
                windows(q, slot, turn, 0)
                if not isinstance(q, int) or q > 0:
                    relu(2 * q - 1, 1)
                windows(q, slot, turn, 1)
                relu(2 * q, 0)
                if not isinstance(q, int) or q > 0:
                    scores(q - 1, 1 - slot)

            roll(dve, pairs, 3, 2, pair_step)
            relu(groups - 1, 1)
            scores(pairs - 1, (pairs - 1) % 2)

            dve.wait_ge(s_score, pairs)
            full = n_edges // P
            if n_edges % P:
                dve.tensor_scalar(cols[:, 4:5], iota_f[:, 0:1], float(n_edges % P), -0.5, ALU.is_lt,
                                  ALU.add).then_inc(s_cast, 1)
                dve.wait_ge(s_cast, 6)
                dve.tensor_scalar(cols[:, 4:5], cols[:, 4:5], 3e38, None, ALU.mult).then_inc(s_cast, 1)
                dve.wait_ge(s_cast, 7)
                dve.tensor_scalar(cols[:, 4:5], cols[:, 4:5], 2.0, None, ALU.mult).then_inc(s_cast, 1)
                dve.wait_ge(s_cast, 8)
                dve.tensor_tensor(score[:, full:full + 1], score[:, full:full + 1], cols[:, 4:5],
                                  ALU.min).then_inc(s_soft, 1)
                full += 1
            else:
                dve.memset(cols[:, 4:5], 0.0).then_inc(s_soft, 1)
            if full < tiles:
                dve.memset(score[:, full:tiles], -3e38).then_inc(s_cast, 1)
                dve.wait_ge(s_cast, 9 if n_edges % P else 6)
            dve.wait_ge(s_soft, 1)
            dve.tensor_reduce(cols[:, 0:1], score[:, :], AX_X, ALU.max).then_inc(s_soft, 1)
            dve.wait_ge(s_max, 1)
            dve.tensor_scalar(cols[:, 2:3], cols[:, 1:2], -1.0 / H, None, ALU.mult).then_inc(s_soft, 1)
            dve.wait_ge(s_exp, 1)
            dve.tensor_scalar(nonzero[:, :], score[:, :], 0.0, None, ALU.not_equal).then_inc(s_soft, 1)
            dve.wait_ge(s_total, 1)
            dve.reciprocal(cols[:, 5:6], pre[0][:, 0:1]).then_inc(s_soft, 1)
            dve.wait_ge(s_counts, 1)
            dve.wait_ge(s_const, 9)
            kp = key_parts
            dve.tensor_scalar(flag[0:kp, :], pre[1][0:kp, 0:key_cols], 0.0, None, ALU.is_gt).then_inc(s_counts, 1)
            dve.tensor_scalar(key[0:kp, :], row_i[0:kp, 0:key_cols], float(-kp), KEY, ALU.mult, ALU.add).then_inc(
                s_counts, 1)
            dve.wait_ge(s_counts, 3)
            dve.tensor_reduce(cols[:, 6:7], flag[:, :], AX_X, ALU.add).then_inc(s_counts, 1)
            dve.tensor_scalar(key[0:kp, :], key[0:kp, :], iota_f[0:kp, 0:1], None, ALU.subtract).then_inc(s_seg_key, 1)
            dve.wait_ge(s_seg_key, 1)
            dve.tensor_tensor(key[:, :], key[:, :], flag[:, :], ALU.mult).then_inc(s_seg_key, 1)
            dve.wait_ge(s_counts, 5)
            dve.tensor_copy(count_i[:, :], cols[0:1, 7:8]).then_inc(s_left, 1)
            dve.wait_ge(s_left, 1)
            dve.wait_ge(s_seg_key, 2)
            left = dve.value_load(count_i[0:1, 0:1], min_val=1, max_val=tiles)

            with dve.Fori(0, left) as i:
                dve.tensor_reduce(cols[:, 8:9], key[:, :], AX_X, ALU.max).then_inc(s_seg_key, 1)
                dve.wait_ge(s_seg_max, i + 1)
                dve.tensor_scalar(tile_i[:, :], cols[0:1, 9:10], -1.0, KEY, ALU.mult, ALU.add).then_inc(s_seg_tile, 1)
                dve.scalar_tensor_tensor(out=key[:, :], in0=key[:, :], scalar=cols[:, 9:10], in1=key[:, :],
                                         op0=ALU.not_equal, op1=ALU.mult).then_inc(s_seg_key, 1)
                dve.wait_ge(s_seg_tile, i + 1)
                dve.sem_inc(s_passed, 1)
                t = dve.value_load(tile_i[0:1, 0:1], min_val=0, max_val=tiles - 1)
                dve.tensor_scalar(seg_f[:, 0:1], score[:, bass.ds(t, 1)], cols[:, 5:6], None, ALU.mult).then_inc(
                    s_seg, 1)
                dve.wait_ge(s_seg_in, 48 * i + 48)
                dve.tensor_copy(seg_f[:, 1:2], seg_col[:, 0:1]).then_inc(s_seg, 1)
                dve.wait_ge(s_seg, 10 * i + 2)
                dve.tensor_scalar(seg_w[:, :], seg_row[:, :], seg_f[:, 1:2], seg_f[:, 0:1], ALU.is_equal,
                                  ALU.mult).then_inc(s_seg, 1)
                dve.wait_ge(s_seg_mm, 2 * i + 1)
                dve.tensor_copy(seg_t[:, :], pre[0][:, 0:P]).then_inc(s_seg, 1)
                dve.scalar_tensor_tensor(out=seg_s[:, :], in0=seg_row[:, :], scalar=seg_f[:, 1:2], in1=before[:, :],
                                         op0=ALU.is_equal, op1=ALU.mult).then_inc(s_seg, 1)
                dve.wait_ge(s_seg, 10 * i + 5)
                dve.tensor_reduce(seg_f[:, 2:3], seg_s[:, :], AX_X, ALU.max).then_inc(s_seg, 1)
                dve.tensor_tensor(seg_f[:, 3:4], iota_f[:, 0:1], seg_f[:, 1:2], ALU.subtract).then_inc(s_seg, 1)
                dve.wait_ge(s_seg, 10 * i + 7)
                dve.tensor_scalar(seg_f[:, 4:5], seg_f[:, 3:4], float(n_pad), seg_f[:, 2:3], ALU.add,
                                  ALU.mult).then_inc(s_seg, 1)
                dve.wait_ge(s_seg, 10 * i + 8)
                dve.tensor_tensor(seg_to[:, :], seg_f[:, 4:5], seg_f[:, 1:2], ALU.add).then_inc(s_seg, 1)
                dve.wait_ge(s_seg_mm, 2 * i + 2)
                dve.tensor_copy(seg_o[:, :], pre[0][:, P:2 * P]).then_inc(s_seg, 1)
                dve.wait_ge(s_seg_add, 16 * i + 16)

            def node_step(c, slot, turn):
                dve.wait_ge(s_h, c + 1)
                dve.wait_ge(s_sum[slot], 16 * (turn + 1))
                wait(dve, s_out[slot], 16 * turn)
                dve.tensor_tensor(y[:, slot, :], wide[slot][:, 0:CW], stage[:, slot, :], ALU.add).then_inc(s_y, 1)
                for n in range(2):
                    if n == 0:
                        dve.wait_ge(s_y, c + 1)
                    else:
                        dve.wait_ge(s_gam, 2 * c + 2)
                        dve.tensor_tensor(y[:, slot, :], y[:, slot, :], x_res[:, bass.ds(c * CW, CW)],
                                          ALU.add).then_inc(s_z, 1)
                        dve.wait_ge(s_z, c + 1)
                    for j in range(CHUNK):
                        last = dve.bn_stats(stats[:, slot, j, :], y[:, slot, j * P:(j + 1) * P])
                    last.then_inc(s_bn, 1)
                    dve.wait_ge(s_bn, 2 * c + n + 1)
                    dve.sem_inc(s_passed, 1)
                    for j in range(CHUNK):
                        last = dve.bn_aggr(moments[:, slot, j, :], stats[:, slot, j, :])
                    last.then_inc(s_stat, 1)
                    dve.wait_ge(s_std, 2 * c + n + 1)
                    dve.reciprocal(rstd[:, slot, :], std[:, slot, :]).then_inc(s_stat, 1)
                    dve.wait_ge(s_stat, 6 * c + 3 * n + 2)
                    dve.scalar_tensor_tensor(out=shift[:, slot, :], in0=moments[:, slot, :, 0], scalar=-1.0,
                                             in1=rstd[:, slot, :], op0=ALU.mult, op1=ALU.mult).then_inc(s_stat, 1)

            roll(dve, chunks, 2, 2, node_step)


_ROWS = ("x_rows", "x_aligned", "x_strided", "edges", "src_pairs", "dst_pairs", "src_tiles", "dst_tiles", "wqT", "wkT",
         "weT", "wv", "wn", "bn", "bq", "bk", "bv", "be", "A1", "b1", "A2", "b2", "gamma", "beta")


def lay_out(x, src, dst, edge_attr_64, **w):
    x, src, dst, edge_attr = (np.asarray(a) for a in (x, src, dst, edge_attr_64))
    w = {k.replace("L0_gnn_", ""): np.asarray(v) for k, v in w.items()}
    n, d = x.shape
    e, de = edge_attr.shape
    step = P * CHUNK
    chunks = -(-n // step)
    chunks += chunks % 2
    pairs = -(-e // PAIR)
    pairs += 1 - pairs % 2
    xp = np.pad(x, ((0, chunks * step - n), (0, 0)))
    ep = np.pad(edge_attr, ((0, pairs * PAIR - e), (0, 0)))
    sp, dp = (np.pad(a, (0, pairs * PAIR - e), mode="edge") for a in (src, dst))
    arrays = {
        "x_rows": xp,
        "x_aligned": xp.reshape(chunks, step, d).transpose(0, 2, 1),
        "x_strided": xp.reshape(P, chunks, CHUNK, d).transpose(1, 3, 2, 0).reshape(chunks, d, step),
        "edges": ep.reshape(pairs, 2, GROUP, de).transpose(0, 1, 3, 2).reshape(pairs, 2 * de, GROUP),
        "src_pairs": sp.reshape(pairs, PT, P).transpose(0, 2, 1),
        "dst_pairs": dp.reshape(pairs, PAIR),
        "src_tiles": sp.reshape(pairs * PT, P),
        "dst_tiles": dp.reshape(pairs * PT, P),
        "wqT": w["Wq"].T, "wkT": w["Wk"].T, "weT": w["We"].T, "wv": w["Wv"], "wn": w["Wn"],
        "bn": w["bn"], "bq": w["bq"], "bk": w["bk"], "bv": w["bv"], "be": w["be"], "A1": w["A1"], "b1": w["b1"],
        "A2": w["A2"], "b2": w["b2"], "gamma": w["gamma"], "beta": w["beta"],
    }
    return {k: np.ascontiguousarray(arrays[k]) for k in _ROWS}


def kernel(**inputs):
    import concourse.bacc as bacc
    from concourse.bass_utils import run_bass_kernel_spmd

    n, d = inputs["x"].shape
    arrays = {f"in_{k}_dram": a for k, a in lay_out(**inputs).items()}
    nc = bacc.Bacc("TRN2", target_bir_lowering=False, num_devices=1)
    args = [nc.dram_tensor(k, a.shape, mybir.dt.from_np(a.dtype), kind="ExternalInput").ap() for k, a in arrays.items()]
    out = nc.dram_tensor("out_0_dram", (arrays["in_x_rows_dram"].shape[0], d), F32, kind="ExternalOutput").ap()
    build(nc, *args, out, inputs["edge_attr_64"].shape[0])
    r = run_bass_kernel_spmd(nc, [arrays], core_ids=[0])
    return r.results[0]["out_0_dram"][:n]
```

```python
from contextlib import ExitStack

import numpy as np
import concourse.bass as bass
from concourse import mybir

F32 = mybir.dt.float32
BF16 = mybir.dt.bfloat16
I32 = mybir.dt.int32
ALU = mybir.AluOpType
ACT = mybir.ActivationFunctionType
AX_X = mybir.AxisListType.X
RED = bass.bass_isa.ReduceOp

P = 128
GROUP = 512
TILES = GROUP // P
PAIR = 2 * GROUP
PT = PAIR // P
CHUNK = 7
EXTRA = 1
SLOPE = 0.2
EPS = 1e-5
MORE = 256
KEY = 8192.0
OUT_MORE = P
BLOCK_LAG = 3
XA = 4


def largest_divisor(n, most):
    return max(d for d in range(1, most + 1) if n % d == 0)


def roll(eng, total, peel, ring, step):
    for n in range(peel):
        step(n, n % ring, n // ring)
    assert (total - peel) % ring == 0
    if total == peel:
        return
    with eng.Fori(0, (total - peel) // ring) as i:
        for u in range(ring):
            n = peel + u
            step(n + ring * i, n % ring, n // ring + i)


def over_pairs(eng, pairs, blocks, pair_step, node_step):
    for q in range(3):
        pair_step(q, q % 2, q // 2)
    total = (pairs - 3) // 2
    with_nodes = blocks + BLOCK_LAG
    assert (pairs - 3) % 2 == 0 and total > with_nodes

    def iteration(i, nodes):
        for u in range(2):
            pair_step(3 + u + 2 * i, (3 + u) % 2, (3 + u) // 2 + i)
            if nodes:
                node_step(i, u)

    for i in range(BLOCK_LAG):
        iteration(i, True)
    with eng.Fori(BLOCK_LAG, blocks) as i:
        iteration(i, True)
    for i in range(blocks, with_nodes):
        iteration(i, True)
    with eng.Fori(with_nodes, total) as i:
        iteration(i, False)


def wait(eng, sem, value):
    if not isinstance(value, int) or value > 0:
        eng.wait_ge(sem, value)


def build(nc, x_rows, x_blocks, x_strided, edges, src_pairs, dst_pairs, src_tiles, dst_tiles, wqT, wkT, weT, wv, wn,
          bn, bq, bk, bv, be, A1, b1, A2, b2, gamma, beta, out, n_edges):
    n_pad, D = x_rows.shape
    H = A2.shape[1]
    DE = weT.shape[1]
    pairs = edges.shape[0]
    groups = 2 * pairs
    tiles = PT * pairs
    chunks, _, CW = x_strided.shape
    blocks = chunks * CHUNK
    assert CW == CHUNK * P and blocks * P == n_pad and D == P and 2 * DE == P and tiles < KEY and blocks <= MORE
    info_parts = largest_divisor(groups, P)
    info_cols = groups // info_parts
    key_parts = largest_divisor(tiles, P)
    key_cols = tiles // key_parts

    pq_dram = nc.dram_tensor("pq_dram", (n_pad, D), F32).ap()
    y_dram = nc.dram_tensor("y_dram", (n_pad + P, D), F32).ap()
    span_dram = nc.dram_tensor("span_dram", (groups, 2), I32).ap()

    with ExitStack() as ctx:
        def sb(name, shape, dt):
            return ctx.enter_context(nc.sbuf_tensor(name, shape, dt))

        def ps(name, shape, dt):
            return ctx.enter_context(nc.psum_tensor(name, shape, dt))

        def sem(name):
            return ctx.enter_context(nc.semaphore(name))

        pk = sb("pk", [P, blocks + EXTRA, 3, P], BF16)
        xa = sb("xa", [P, XA, CW], F32)
        stage = sb("stage", [P, 2, CW], F32)
        pk_rest = sb("pk_rest", [P, 2, CW], F32)
        w_in = sb("w_in", [P, 2, P], F32)
        we_in = sb("we_in", [P, 2, P], F32)
        a1_in = sb("a1_in", [P, 3, P], F32)
        wv_sb = sb("wv_sb", [P, P], F32)
        wn_sb = sb("wn_sb", [P, P], F32)
        a2_sb = sb("a2_sb", [P, H], F32)
        bcols = sb("bcols", [P, 4], F32)
        b2_row = sb("b2_row", [P, H], F32)
        bv_row = sb("bv_row", [P, P], F32)
        bn_row = sb("bn_row", [P, P], F32)
        gamma_row = sb("gamma_row", [P, P], F32)
        beta_row = sb("beta_row", [P, P], F32)
        w_fold = sb("w_fold", [P, 4, P], F32)
        bias_col = sb("bias_col", [P, 2], F32)
        iota_i = sb("iota_i", [P, P], I32)
        iota_f = sb("iota_f", [P, P], F32)
        row_i = sb("row_i", [P, P], I32)
        ident = sb("ident", [P, P], F32)
        before = sb("before", [P, P], F32)
        ones_f = sb("ones_f", [P, P], F32)
        ones_b = sb("ones_b", [P, 1], BF16)
        spans = sb("spans", [info_parts, 8, info_cols], I32)
        span_row = sb("span_row", [1, groups, 2], I32)
        rounds_f = sb("rounds_f", [1, groups], F32)
        sums_f = sb("sums_f", [1, groups], F32)
        zeros_f = sb("zeros_f", [1, groups], F32)
        info = sb("info", [1, groups, 4], I32)
        edge = sb("edge", [P, 2, GROUP], F32)
        dst_b = sb("dst_b", [P, 2, PAIR], I32)
        src_i = sb("src_i", [P, 2, PT], I32)
        rows = sb("rows", [P, 4, TILES, P], F32)
        onehot = sb("onehot", [P, 2, GROUP], BF16)
        extra = sb("extra", [P, EXTRA, GROUP], BF16)
        sloped = sb("sloped", [P, 2, GROUP], F32)
        hidden = sb("hidden", [P, 2, GROUP], F32)
        head_b = sb("head_b", [P, PT, H], F32)
        head_l = sb("head_l", [P, PT, H], F32)
        score = sb("score", [P, tiles], F32)
        cols = sb("cols", [P, 16], F32)
        nonzero = sb("nonzero", [P, tiles], BF16)
        key = sb("key", [P, key_cols], F32)
        flag = sb("flag", [P, key_cols], F32)
        count_i = sb("count_i", [1, 1], I32)
        tile_i = sb("tile_i", [1, 1], I32)
        seg_row = sb("seg_row", [P, P], I32)
        seg_col = sb("seg_col", [P, 2], I32)
        seg_f = sb("seg_f", [P, 8], F32)
        seg_to = sb("seg_to", [P, 1], I32)
        seg_x = sb("seg_x", [P, P], F32)
        seg_w = sb("seg_w", [P, P], F32)
        seg_s = sb("seg_s", [P, P], F32)
        seg_t = sb("seg_t", [P, P], F32)
        seg_o = sb("seg_o", [P, P], F32)
        seg_y = sb("seg_y", [P, P], F32)
        seg_xs = sb("seg_xs", [P, P], F32)
        seg_st = sb("seg_st", [P, 2, 6], F32)
        seg_m = sb("seg_m", [P, 2, 4], F32)
        node_x = sb("node_x", [P, P], F32)
        node_r = sb("node_r", [P, P], F32)
        node_y = sb("node_y", [P, P], F32)
        node_t = sb("node_t", [P, P], F32)
        node_o = sb("node_o", [P, P], F32)
        node_st = sb("node_st", [P, 2, 6], F32)
        node_m = sb("node_m", [P, 2, 4], F32)
        pk_words = pk[:, :, :, :].rearrange("p b c n -> p (b c n)").bitcast(F32)
        span_in = pk_words[0:info_parts, 0:info_cols * GROUP].bitcast(I32)

        wide = [ps(f"wide{i}", [P, 1024], F32) for i in range(2)]
        pre = [ps(f"pre{i}", [P, GROUP], F32) for i in range(2)]
        heads = [ps(f"heads{i}", [P, 512], F32) for i in range(2)]

        s_weights = sem("weights_loaded")
        s_passed = sem("passed")
        s_const = sem("constants_made")
        s_bias_col = sem("bias_column_ready")
        s_fold = sem("weights_folded")
        s_folded = sem("folded_copied")
        s_iota = sem("iota_made")
        s_cast = sem("constants_cast")
        s_span_in = sem("dst_for_spans_loaded")
        s_span = sem("span_steps")
        s_span_out = sem("spans_stored")
        s_span_row = sem("spans_back")
        s_info = sem("info_steps")
        s_xa = [sem(f"nodes_loaded{i}") for i in range(XA)]
        s_pq_mm = sem("pq_products")
        s_pq_stage = sem("pq_staged")
        s_pq_out = [sem(f"pq_stored{i}") for i in range(2)]
        s_xk = [sem(f"nodes_loaded_again{i}") for i in range(XA)]
        s_pk_mm = sem("pk_products")
        s_pk_hi = sem("pk_high_made")
        s_pk_rest = sem("pk_rest_made")
        s_pk_mid = sem("pk_mid_made")
        s_pk_lo = sem("pk_low_made")
        s_first = sem("first_weights_loaded")
        s_bias = sem("biases_loaded")
        s_late = sem("node_weights_loaded")
        s_y_init = sem("rows_behind_y_written")
        s_edge = [sem(f"edges_loaded{i}") for i in range(2)]
        s_dst = [sem(f"dst_loaded{i}") for i in range(2)]
        s_src = [sem(f"src_loaded{i}") for i in range(2)]
        s_rows = [sem(f"rows_gathered{i}") for i in range(4)]
        s_edge_used = sem("edges_used")
        s_onehot = sem("onehot_ready")
        s_extra = sem("extra_onehots_ready")
        s_extra_used = sem("extra_onehots_used")
        s_pre = sem("pre_ready")
        s_sloped = sem("sloped_ready")
        s_hidden = sem("hidden_ready")
        s_heads = sem("heads_ready")
        s_head_b = sem("heads_biased")
        s_head_l = sem("heads_relued")
        s_score = sem("scores_ready")
        s_soft = sem("softmax_steps")
        s_max = sem("maximum_ready")
        s_exp = sem("exponentials_ready")
        s_total = sem("total_ready")
        s_counts = sem("tile_counts_ready")
        s_left = sem("tiles_counted")
        s_seg_key = sem("segment_key_steps")
        s_seg_max = sem("segment_key_reduced")
        s_seg_tile = sem("segment_tile_known")
        s_seg_in = sem("segment_indices_loaded")
        s_seg_x = sem("segment_rows_gathered")
        s_seg = sem("segment_steps")
        s_seg_mm = sem("segment_products")
        s_seg_add = sem("segment_added")
        s_seg_y = sem("segment_y_gathered")
        s_seg_ln = sem("segment_norm_steps")
        s_seg_sd = sem("segment_deviations")
        s_seg_out = sem("segment_rows_stored")
        s_node_x = sem("node_columns_loaded")
        s_node_r = sem("node_rows_loaded")
        s_node_h = sem("node_products")
        s_node_y = sem("node_y_ready")
        s_node_y_out = sem("node_y_stored")
        s_node_st = [sem(f"node_stats{n}") for n in range(2)]
        s_node_m = [sem(f"node_moments{n}") for n in range(2)]
        s_node_sd = [sem(f"node_deviations{n}") for n in range(2)]
        s_node_inv = [sem(f"node_inverse_deviations{n}") for n in range(2)]
        s_node_t = sem("node_first_norm_steps")
        s_node_o = sem("node_result_ready")
        s_node_out = sem("node_result_stored")

        pq_chunks = pq_dram.rearrange("(p c j) d -> c p (j d)", c=chunks, j=CHUNK)
        y_blocks = y_dram.rearrange("(b p) d -> b p d", p=P)
        out_blocks = out.rearrange("(b p) d -> b p d", p=P)
        x_row_blocks = x_rows.rearrange("(b p) d -> b p d", p=P)
        EDGE_WEIGHTS, NODE_WEIGHTS = 5, 6

        def valid(b):
            return not isinstance(b, int) or 0 <= b < blocks

        def info_of(eng, g, n, most):
            return eng.value_load(info[0:1, bass.ds(g, 1), n:n + 1].rearrange("a b c -> a (b c)"), min_val=0,
                                  max_val=most)

        def word_of(eng, q):
            return info_of(eng, 2 * q, 3, 4 * MORE * MORE - 1)

        def window_of(eng, word, h):
            part = word & (2 * MORE - 1) if h == 0 else word >> (2 * MORE).bit_length() - 1
            return (part & (MORE - 1)).with_bounds(min_val=0, max_val=blocks - 1), part >> MORE.bit_length() - 1

        def rounds_of(eng, g):
            return info_of(eng, g, 1, blocks // EXTRA + 1), info_of(eng, g, 2, groups * (blocks // EXTRA + 1))

        MADE = 9

        block = ctx.enter_context(nc.Block())

        @block.sync
        def _(sp):
            sp.dma_start(w_in[:, 0, :], wqT).then_inc(s_first, 16)
            sp.dma_start(a1_in[:, :, :], A1.rearrange("(c p) n -> p c n", p=P)).then_inc(s_first, 16)

            def pq_step(c, slot, turn):
                wait(sp, s_pq_mm, c - XA + 1)
                sp.dma_start(xa[:, slot, :], x_strided[bass.ds(c, 1), :, :].rearrange("a p n -> (a p) n")).then_inc(
                    s_xa[slot], 16)

            roll(sp, chunks, XA + (chunks - XA) % XA, XA, pq_step)

            def pk_load(c, slot):
                sp.dma_start(xa[:, slot, :].rearrange("p (j n) -> p j n", j=CHUNK),
                             x_blocks[bass.ds(c * CHUNK, CHUNK), :, :].rearrange("j p n -> p j n")).then_inc(
                    s_xk[slot], 16)

            def pair_step(q, slot, turn):
                wait(sp, s_hidden, 2 * q - 3)
                sp.dma_start(dst_b[:, slot, :],
                             dst_pairs[bass.ds(q, 1), :].to_broadcast([P, PAIR])).then_inc(s_dst[slot], 16)
                wait(sp, s_edge_used, q - 1)
                sp.dma_start(edge[:, slot, :], edges[bass.ds(q, 1), :, :].rearrange("a p n -> (a p) n")).then_inc(
                    s_edge[slot], 16)
                for h in range(2):
                    wait(sp, s_rows[2 * slot + h], 64 * turn)
                sp.dma_start(src_i[:, slot, :], src_pairs[bass.ds(q, 1), :, :].rearrange("a p n -> (a p) n")).then_inc(
                    s_src[slot], 16)

            pair_step(0, 0, 0)
            pair_step(1, 1, 0)

            for c in range(XA):
                sp.wait_ge(s_pq_mm, chunks)
                pk_load(c, c)

            def pk_step(c, slot, turn):
                wait(sp, s_pk_mm, c - XA + 1)
                pk_load(c, slot)

            roll(sp, chunks, XA + (chunks - XA) % XA, XA,
                 lambda c, slot, turn: None if isinstance(c, int) and c < XA else pk_step(c, slot, turn))

            def node_step(i, u):
                if u == 1 and valid(i):
                    wait(sp, s_node_h, i)
                    sp.dma_start(node_x[:, :], x_blocks[bass.ds(i, 1), :, :].rearrange("a p n -> (a p) n")).then_inc(
                        s_node_x, 16)
                if u == 1 and valid(i - 1):
                    wait(sp, s_node_t, 4 * (i - 1))
                    sp.dma_start(node_r[:, :],
                                 x_row_blocks[bass.ds(i - 1, 1), :, :].rearrange("a p n -> (a p) n")).then_inc(
                        s_node_r, 16)
                if u == 0 and valid(i - 2):
                    wait(sp, s_node_y, i - 1)
                    sp.dma_start(y_blocks[bass.ds(i - 2, 1), :, :].rearrange("a p n -> (a p) n"),
                                 node_y[:, :]).then_inc(s_node_y_out, 16)
                if u == 0 and valid(i - 3):
                    wait(sp, s_node_o, i - 2)
                    sp.dma_start(out_blocks[bass.ds(i - 3, 1), :, :].rearrange("a p n -> (a p) n"),
                                 node_o[:, :]).then_inc(s_node_out, 16)

            over_pairs(sp, pairs, blocks, lambda q, slot, turn: None if isinstance(q, int) and q < 2 else
                       pair_step(q, slot, turn), node_step)

            sp.wait_ge(s_left, 1)
            left = sp.value_load(count_i[0:1, 0:1], min_val=1, max_val=tiles)
            with sp.Fori(0, left) as i:
                sp.wait_ge(s_seg_tile, i + 1)
                sp.sem_inc(s_passed, 1)
                t = sp.value_load(tile_i[0:1, 0:1], min_val=0, max_val=tiles - 1)
                sp.dma_start(seg_row[:, :], src_tiles[bass.ds(t, 1), :].to_broadcast([P, P])).then_inc(s_seg_in, 16)
                with nc.allow_non_contiguous_dma(reason="one index per partition"):
                    sp.dma_start(seg_col[:, 0:1], src_tiles[bass.ds(t, 1), :].rearrange("a p -> p a")).then_inc(
                        s_seg_in, 16)
                    sp.dma_start(seg_col[:, 1:2], dst_tiles[bass.ds(t, 1), :].rearrange("a p -> p a")).then_inc(
                        s_seg_in, 16)

            sp.wait_ge(s_node_out, 16 * blocks)
            sp.wait_ge(s_seg_out, 16 * left)
            sp.sem_inc(s_passed, 1)

        @block.gpsimd
        def _(pool):
            pool.iota(iota_i[:, :], [[P, P]], base=0, channel_multiplier=1).then_inc(s_iota, 1)
            pool.iota(row_i[:, :], [[1, P]], base=0, channel_multiplier=0).then_inc(s_iota, 1)
            pool.memset(ones_f[:, :], 1.0).then_inc(s_const, 1)
            pool.memset(ident[:, :], 0.0).then_inc(s_const, 1)
            pool.memset(ones_b[:, :], 1.0).then_inc(s_const, 1)
            pool.memset(zeros_f[:, :], 0.0).then_inc(s_const, 1)
            pool.memset(info[:, :, :], 0).then_inc(s_const, 1)
            pool.wait_ge(s_const, 5)
            pool.affine_select(out=ident[:, :], in_=ident[:, :], compare_op=ALU.not_equal, fill=1.0, base=0,
                               pattern=[[-1, P]], channel_multiplier=1).then_inc(s_const, 1)
            pool.affine_select(out=before[:, :], in_=ones_f[:, :], compare_op=ALU.is_gt, fill=0.0, base=0,
                               pattern=[[-1, P]], channel_multiplier=1).then_inc(s_const, 1)
            pool.memset(key[:, :], 0.0).then_inc(s_const, 1)
            pool.memset(flag[:, :], 0.0).then_inc(s_const, 1)

            for slot in range(2):
                pool.wait_ge(s_pq_out[slot], 16 * (chunks // 2))

            def pair_step(q, slot, turn):
                for h in range(2):
                    if h == 0:
                        pool.wait_ge(s_src[slot], 16 * (turn + 1))
                    wait(pool, s_pre, 2 * q + h - 3)
                    pool.sem_inc(s_passed, 1)
                    for k in range(TILES):
                        pool.indirect_dma_start(
                            rows[:, 2 * slot + h, k, :], None, pq_dram,
                            bass.IndirectOffsetOnAxis(src_i[:, slot, h * TILES + k:h * TILES + k + 1], 0),
                        ).then_inc(s_rows[2 * slot + h], 16)

            roll(pool, pairs, 3, 2, pair_step)

            pool.wait_ge(s_soft, 2)
            pool.partition_all_reduce(cols[:, 1:2], cols[:, 0:1], P, RED.max).then_inc(s_max, 1)
            pool.wait_ge(s_counts, 4)
            pool.partition_all_reduce(cols[:, 7:8], cols[:, 6:7], P, RED.add).then_inc(s_counts, 1)

            pool.wait_ge(s_left, 1)
            pool.wait_ge(s_y_init, 16)
            pool.wait_ge(s_node_y_out, 16 * blocks)
            pool.wait_ge(s_node_out, 16 * blocks)
            left = pool.value_load(count_i[0:1, 0:1], min_val=1, max_val=tiles)
            with pool.Fori(0, left) as i:
                pool.wait_ge(s_seg_key, 2 * i + 3)
                pool.sem_inc(s_passed, 1)
                pool.partition_all_reduce(cols[:, 9:10], cols[:, 8:9], P, RED.max).then_inc(s_seg_max, 1)
                pool.wait_ge(s_seg_in, 48 * i + 48)
                pool.sem_inc(s_passed, 1)
                pool.indirect_dma_start(seg_x[:, :], None, x_rows,
                                        bass.IndirectOffsetOnAxis(seg_col[:, 1:2], 0)).then_inc(s_seg_x, 16)
                pool.wait_ge(s_seg, 10 * i + 10)
                pool.sem_inc(s_passed, 1)
                pool.indirect_dma_start(y_dram, bass.IndirectOffsetOnAxis(seg_to[:, 0:1], 0), seg_o[:, :], None,
                                        compute_op=ALU.add).then_inc(s_seg_add, 16)
                pool.indirect_dma_start(seg_xs[:, :], None, x_rows,
                                        bass.IndirectOffsetOnAxis(seg_col[:, 0:1], 0)).then_inc(s_seg_y, 16)
                pool.wait_ge(s_seg_add, 16 * i + 16)
                pool.sem_inc(s_passed, 1)
                pool.indirect_dma_start(seg_y[:, :], None, y_dram,
                                        bass.IndirectOffsetOnAxis(seg_col[:, 0:1], 0)).then_inc(s_seg_y, 16)
                pool.wait_ge(s_seg_ln, 11 * i + 11)
                pool.sem_inc(s_passed, 1)
                pool.indirect_dma_start(out, bass.IndirectOffsetOnAxis(seg_to[:, 0:1], 0), seg_o[:, :],
                                        None).then_inc(s_seg_out, 16)
                pool.wait_ge(s_seg_out, 16 * i + 16)

        @block.scalar
        def _(act):
            def row_of(t, b, s):
                act.dma_start(t[:, :], b.rearrange("(a n) -> a n", a=1).to_broadcast([P, b.shape[0]])).then_inc(s, 16)

            for n, b in enumerate((bq, bk, be, b1)):
                act.dma_start(bcols[:, n:n + 1], b.rearrange("(p a) -> p a", a=1)).then_inc(s_bias, 16)
            act.dma_start(span_in, dst_pairs.rearrange("a n -> (a n)").rearrange("(p m) -> p m", p=info_parts)).then_inc(
                s_span_in, 16)
            act.dma_start(w_in[:, 1, :], wkT).then_inc(s_weights, 16)
            act.dma_start(we_in[:, 0, 0:DE], weT).then_inc(s_weights, 16)
            act.dma_start(we_in[:, 1, DE:P], weT).then_inc(s_weights, 16)
            act.dma_start(a2_sb[:, :], A2).then_inc(s_weights, 16)
            row_of(b2_row, b2, s_weights)

            def pq_store(c, slot, turn):
                act.wait_ge(s_pq_mm, c + 1)
                wait(act, s_pq_out[slot], 16 * turn)
                act.copy(stage[:, slot, :], wide[slot][:, 0:CW]).then_inc(s_pq_stage, 1)
                act.wait_ge(s_pq_stage, c + 1)
                act.dma_start(pq_chunks[bass.ds(c, 1), :, :].rearrange("a p n -> (a p) n"),
                              stage[:, slot, :]).then_inc(s_pq_out[slot], 16)

            roll(act, chunks, 2, 2, pq_store)

            act.dma_start(wv_sb[:, :], wv).then_inc(s_late, 16)
            act.dma_start(wn_sb[:, :], wn).then_inc(s_late, 16)
            for t, b in ((bv_row, bv), (bn_row, bn), (gamma_row, gamma), (beta_row, beta)):
                row_of(t, b, s_late)

            act.wait_ge(s_span, 7)
            act.dma_start(span_dram.rearrange("(p g) c -> p (g c)", p=info_parts),
                          spans[:, 6:8, :].rearrange("p a b -> p (a b)")).then_inc(s_span_out, 16)
            act.wait_ge(s_span_out, 16)
            act.dma_start(span_row[:, :, :], span_dram.rearrange("(a g) c -> a g c", a=1)).then_inc(s_span_row, 16)

            act.wait_ge(s_span, 2)

            def pk_step(c, slot, turn):
                act.wait_ge(s_pk_mm, c + 1)
                act.copy(pk[:, bass.ds(c * CHUNK, CHUNK), 0, :],
                         wide[slot][:, 0:CW].rearrange("p (j d) -> p j d", j=CHUNK)).then_inc(s_pk_hi, 1)
                act.wait_ge(s_pk_rest, c + 1)
                act.copy(pk[:, bass.ds(c * CHUNK, CHUNK), 1, :],
                         pk_rest[:, slot, :].rearrange("p (j d) -> p j d", j=CHUNK)).then_inc(s_pk_mid, 1)

            roll(act, chunks, 2, 2, pk_step)

            act.wait_ge(s_bias_col, 1)
            act.wait_ge(s_late, 16 * NODE_WEIGHTS)
            act.dma_start(y_dram[n_pad:n_pad + P, :], bn_row[:, :]).then_inc(s_y_init, 16)

            def pair_step(q, slot, turn):
                for h in range(2):
                    act.wait_ge(s_pre, 2 * q + h + 1)
                    wait(act, s_hidden, 2 * q + h - 1)
                    act.activation(sloped[:, h, :], pre[h][:, :], ACT.Identity, bias=bias_col[:, 1:2],
                                   scale=SLOPE).then_inc(s_sloped, 1)

            def node_step(i, u):
                n, b = (1, i - 1) if u == 0 else (0, i)
                if valid(b):
                    act.wait_ge(s_node_m[n], b + 1)
                    act.activation(node_m[:, n, 2:3], node_m[:, n, 1:2], ACT.Sqrt, bias=cols[:, 12:13]).then_inc(
                        s_node_sd[n], 1)

            over_pairs(act, pairs, blocks, pair_step, node_step)

            act.wait_ge(s_soft, 3)
            act.activation(score[:, :], score[:, :], ACT.Exp, bias=cols[:, 2:3], scale=1.0 / H,
                           accum_out=cols[:, 3:4]).then_inc(s_exp, 1)

            act.wait_ge(s_left, 1)
            left = act.value_load(count_i[0:1, 0:1], min_val=1, max_val=tiles)
            with act.Fori(0, left) as i:
                for n in range(2):
                    act.wait_ge(s_seg_ln, 11 * i + (2, 9)[n])
                    act.activation(seg_m[:, n, 2:3], seg_m[:, n, 1:2], ACT.Sqrt, bias=cols[:, 12:13]).then_inc(
                        s_seg_sd, 1)

        @block.tensor
        def _(pe):
            fold = wide[0][:, 0:512].rearrange("p (c n) -> p c n", c=4)
            pe.wait_ge(s_first, 32)
            pe.matmul(fold[:, 0, :], w_in[:, 0, :], a1_in[:, 0, :], start=True, stop=True).then_inc(s_fold, 1)
            pe.wait_ge(s_bias, 64)
            for n in range(3):
                last = pe.matmul(wide[1][:, 0:1], a1_in[:, n, :], bcols[:, n:n + 1], start=(n == 0), stop=(n == 2))
            last.then_inc(s_fold, 1)
            pe.wait_ge(s_folded, 2)

            def table(c, slot, turn, which, loaded, done, free_sem, free):
                pe.wait_ge(loaded[slot], 16 * (turn + 1))
                wait(pe, free_sem, free)
                for j in range(CHUNK):
                    last = pe.matmul(wide[slot % 2][:, j * P:(j + 1) * P], xa[:, slot, j * P:(j + 1) * P],
                                     w_fold[:, which, :], start=True, stop=True)
                last.then_inc(done, 1)

            roll(pe, chunks, XA + (chunks - XA) % XA, XA, lambda c, slot, turn: table(c, slot, turn, 0, s_xa, s_pq_mm, s_pq_stage, c - 1))
            pe.wait_ge(s_pq_stage, chunks)
            pe.wait_ge(s_weights, 16 * EDGE_WEIGHTS)
            pe.wait_ge(s_cast, 2)
            pe.matmul(fold[:, 1, :], w_in[:, 1, :], a1_in[:, 1, :], start=True, stop=True)
            pe.matmul(fold[:, 2, :], we_in[:, 0, :], a1_in[:, 2, :], start=True, stop=True)
            pe.matmul(fold[:, 3, :], we_in[:, 1, :], a1_in[:, 2, :], start=True, stop=True).then_inc(s_fold, 1)
            pe.wait_ge(s_folded, 3)
            roll(pe, chunks, XA + (chunks - XA) % XA, XA, lambda c, slot, turn: table(c, slot, turn, 1, s_xk, s_pk_mm, s_pk_rest, c - 1))

            pe.wait_ge(s_pk_lo, chunks)
            pe.wait_ge(s_pk_hi, chunks)
            pe.wait_ge(s_info, 7)
            pe.sem_inc(s_extra_used, 1)
            flat = pk[:, :, :, :].rearrange("p b c n -> p (b c n)")

            def score_mm(h, slot):
                for k in range(TILES):
                    at = (h * TILES + k) * H
                    last = pe.matmul(heads[slot][:, at:at + H], hidden[:, h, k * P:(k + 1) * P], a2_sb[:, :],
                                     start=True, stop=True)
                last.then_inc(s_heads, 1)

            def pair_step(q, slot, turn):
                word = word_of(pe, q)
                for h in range(2):
                    g = 2 * q + h
                    first, more = window_of(pe, word, h)
                    if h == 0:
                        pe.wait_ge(s_edge[slot], 16 * (turn + 1))
                    wait(pe, s_hidden, g - 1)
                    product = pe.matmul(pre[h][:, :], w_fold[:, 2 + h, :], edge[:, slot, :], start=True, stop=False,
                                        skip_group_check=True)
                    if h == 1:
                        product.then_inc(s_edge_used, 1)
                    pe.wait_ge(s_onehot, g + 1)
                    for c in range(3):
                        pe.matmul(pre[h][:, :], flat[:, bass.ds(first * (3 * P) + c * P, P)], onehot[:, h, :],
                                  start=False, stop=False, skip_group_check=True)
                    with pe.If(more > 0):
                        n_extra, n_before = rounds_of(pe, g)
                        with pe.Fori(0, n_extra) as r:
                            pe.wait_ge(s_extra, n_before + r + 1)
                            done = (first + r * EXTRA).with_bounds(min_val=0, max_val=blocks - 1)
                            for w in range(EXTRA):
                                for c in range(3):
                                    at = done * (3 * P) + (1 + w) * 3 * P + c * P
                                    last = pe.matmul(pre[h][:, :], flat[:, bass.ds(at, P)], extra[:, w, :],
                                                     start=False, stop=False, skip_group_check=True)
                            last.then_inc(s_extra_used, 1)
                    pe.wait_ge(s_rows[2 * slot + h], 64 * (turn + 1))
                    for k in range(TILES):
                        last = pe.matmul(pre[h][:, k * P:(k + 1) * P], rows[:, 2 * slot + h, k, :], ident[:, :],
                                         start=False, stop=True, skip_group_check=True)
                    last.then_inc(s_pre, 1)
                    if h == 1:
                        pe.wait_ge(s_hidden, g)
                        wait(pe, s_head_b, q - 1)
                        score_mm(0, slot)
                    elif not isinstance(q, int) or q > 0:
                        pe.wait_ge(s_hidden, g)
                        score_mm(1, 1 - slot)

            def node_step(i, u):
                if u == 0 and valid(i):
                    if isinstance(i, int) and i == 0:
                        pe.wait_ge(s_late, 16 * NODE_WEIGHTS)
                    pe.wait_ge(s_node_x, 16 * (i + 1))
                    wait(pe, s_node_y, i)
                    pe.matmul(wide[0][:, 0:P], node_x[:, :], wn_sb[:, :], start=True, stop=True).then_inc(s_node_h, 1)

            over_pairs(pe, pairs, blocks, pair_step, node_step)
            pe.wait_ge(s_hidden, groups)
            score_mm(1, (pairs - 1) % 2)

            pe.wait_ge(s_exp, 1)
            pe.matmul(pre[0][:, 0:1], ones_f[:, :], cols[:, 3:4], start=True, stop=True).then_inc(s_total, 1)
            pe.wait_ge(s_soft, 4)
            for c in range(key_cols):
                last = pe.matmul(pre[1][0:key_parts, c:c + 1], nonzero[:, c * key_parts:(c + 1) * key_parts],
                                 ones_b[:, :], start=True, stop=True)
            last.then_inc(s_counts, 1)

            pe.wait_ge(s_left, 1)
            left = pe.value_load(count_i[0:1, 0:1], min_val=1, max_val=tiles)
            with pe.Fori(0, left) as i:
                pe.wait_ge(s_seg_x, 16 * i + 16)
                pe.wait_ge(s_seg, 10 * i + 3)
                pe.matmul(pre[0][:, 0:P], seg_x[:, :], seg_w[:, :], start=True, stop=True).then_inc(s_seg_mm, 1)
                pe.wait_ge(s_seg, 10 * i + 4)
                pe.matmul(pre[0][:, P:2 * P], seg_t[:, :], wv_sb[:, :], start=True, stop=False)
                pe.matmul(pre[0][:, P:2 * P], seg_w[:, :], bv_row[:, :], start=False, stop=True).then_inc(s_seg_mm, 1)

        @block.vector
        def _(dve):
            dve.memset(we_in[:, 0, DE:P], 0.0).then_inc(s_cast, 1)
            dve.memset(we_in[:, 1, 0:DE], 0.0).then_inc(s_cast, 1)
            dve.wait_ge(s_iota, 2)
            dve.tensor_copy(iota_f[:, :], iota_i[:, :]).then_inc(s_cast, 1)
            dve.memset(cols[:, 12:13], EPS).then_inc(s_cast, 1)
            dve.wait_ge(s_const, MADE)
            dve.wait_ge(s_fold, 1)
            dve.tensor_copy(w_fold[:, 0, :], wide[0][:, 0:P]).then_inc(s_folded, 1)
            dve.wait_ge(s_fold, 2)
            dve.tensor_tensor(bias_col[:, 0:1], wide[1][:, 0:1], bcols[:, 3:4], ALU.add).then_inc(s_folded, 1)
            dve.wait_ge(s_folded, 2)
            dve.tensor_scalar(bias_col[:, 1:2], bias_col[:, 0:1], SLOPE, None, ALU.mult).then_inc(s_bias_col, 1)

            dve.wait_ge(s_span_in, 16)
            sv = span_in.rearrange("p (g n) -> p g n", g=info_cols)
            dve.tensor_reduce(spans[:, 0, :], sv, AX_X, ALU.min).then_inc(s_span, 1)
            dve.tensor_reduce(spans[:, 1, :], sv, AX_X, ALU.max).then_inc(s_span, 1)

            dve.wait_ge(s_fold, 3)
            dve.tensor_copy(w_fold[:, 1:4, :], wide[0][:, P:4 * P].rearrange("p (c n) -> p c n", c=3)).then_inc(
                s_folded, 1)

            dve.wait_ge(s_span, 2)
            dve.tensor_scalar(spans[:, 2:4, :], spans[:, 0:2, :], 7, None, ALU.logical_shift_right).then_inc(s_span, 1)
            dve.wait_ge(s_span, 3)
            dve.tensor_tensor(spans[:, 4, :], spans[:, 3, :], spans[:, 2, :], ALU.subtract).then_inc(s_span, 1)
            dve.wait_ge(s_span, 4)
            scale = (1 << 16) // EXTRA + 1
            dve.tensor_scalar(spans[:, 5, :], spans[:, 4, :], float(EXTRA - 1), float(scale), ALU.add,
                              ALU.mult).then_inc(s_span, 1)
            dve.wait_ge(s_span, 5)
            both = spans[:, 6:8, :].rearrange("p a b -> p (a b)").rearrange("p (g c) -> p g c", c=2)
            dve.tensor_copy(both[:, :, 0], spans[:, 2, :]).then_inc(s_span, 1)
            dve.tensor_scalar(both[:, :, 1], spans[:, 5, :], 16, None, ALU.logical_shift_right).then_inc(s_span, 1)

            dve.memset(pk[:, blocks:blocks + EXTRA, :, :], 0.0).then_inc(s_cast, 1)

            def pk_step(c, slot, turn):
                dve.wait_ge(s_pk_hi, c + 1)
                hi = pk[:, bass.ds(c * CHUNK, CHUNK), 0, :]
                rest = pk_rest[:, slot, :].rearrange("p (j d) -> p j d", j=CHUNK)
                dve.tensor_tensor(rest, wide[slot][:, 0:CW].rearrange("p (j d) -> p j d", j=CHUNK), hi,
                                  ALU.subtract).then_inc(s_pk_rest, 1)
                dve.wait_ge(s_pk_mid, c + 1)
                mid = pk[:, bass.ds(c * CHUNK, CHUNK), 1, :]
                dve.tensor_tensor(pk[:, bass.ds(c * CHUNK, CHUNK), 2, :], rest, mid, ALU.subtract).then_inc(s_pk_lo, 1)

            roll(dve, chunks, 2, 2, pk_step)

            dve.wait_ge(s_span_row, 16)
            dve.tensor_copy(rounds_f[:, :], span_row[:, :, 1]).then_inc(s_info, 1)
            dve.wait_ge(s_info, 1)
            dve.wait_ge(s_const, 5)
            dve.tensor_tensor_scan(sums_f[:, :], rounds_f[:, :], zeros_f[:, :], 0.0, ALU.add, ALU.add).then_inc(
                s_info, 1)
            dve.wait_ge(s_info, 2)
            dve.tensor_copy(info[:, :, 0:2], span_row[:, :, :]).then_inc(s_info, 1)
            dve.tensor_tensor(info[:, :, 2], sums_f[:, :], rounds_f[:, :], ALU.subtract).then_inc(s_info, 1)
            dve.wait_ge(s_info, 4)
            dve.tensor_scalar(rounds_f[:, :], rounds_f[:, :], 1.0, float(MORE), ALU.min, ALU.mult).then_inc(s_info, 1)
            dve.wait_ge(s_info, 5)
            dve.tensor_tensor(sums_f[:, :], rounds_f[:, :], info[:, :, 0], ALU.add).then_inc(s_info, 1)
            dve.wait_ge(s_info, 6)
            of_pair = sums_f[:, :].rearrange("a (q h) -> a q h", h=2)
            dve.scalar_tensor_tensor(out=info[:, :, 3].rearrange("a (q h) -> a q h", h=2)[:, :, 0],
                                     in0=of_pair[:, :, 1], scalar=2.0 * MORE, in1=of_pair[:, :, 0], op0=ALU.mult,
                                     op1=ALU.add).then_inc(s_info, 1)
            dve.wait_ge(s_info, 7)
            dve.wait_ge(s_weights, 16 * EDGE_WEIGHTS)

            def windows(q, slot, turn, h, word):
                    g = 2 * q + h
                    dst = dst_b[:, slot, h * GROUP:(h + 1) * GROUP]
                    first, more = window_of(dve, word, h)
                    if h == 0:
                        dve.wait_ge(s_dst[slot], 16 * (turn + 1))
                    wait(dve, s_pre, g - 1)
                    dve.tensor_scalar(onehot[:, h, :], dst, iota_f[:, bass.ds(first, 1)], None,
                                      ALU.is_equal).then_inc(s_onehot, 1)
                    with dve.If(more > 0):
                        n_extra, n_before = rounds_of(dve, g)
                        with dve.Fori(0, n_extra) as r:
                            dve.wait_ge(s_extra_used, n_before + r + 1)
                            done = (first + r * EXTRA).with_bounds(min_val=0, max_val=blocks - 1)
                            for w in range(EXTRA):
                                last = dve.tensor_scalar(extra[:, w, :], dst,
                                                         iota_f[:, bass.ds(done + (1 + w), 1)], None,
                                                         ALU.is_equal)
                            last.then_inc(s_extra, 1)

            def relu(g, h):
                dve.wait_ge(s_sloped, g + 1)
                wait(dve, s_heads, g - 1)
                dve.scalar_tensor_tensor(out=hidden[:, h, :], in0=pre[h][:, :], scalar=bias_col[:, 0:1],
                                         in1=sloped[:, h, :], op0=ALU.add, op1=ALU.max).then_inc(s_hidden, 1)

            def scores(q, slot):
                dve.wait_ge(s_heads, 2 * q + 2)
                dve.tensor_tensor(head_b[:, :, :], heads[slot][:, 0:PT * H].rearrange("p (t h) -> p t h", h=H),
                                  b2_row[:, None, :].to_broadcast([P, PT, H]), ALU.add).then_inc(s_head_b, 1)
                dve.wait_ge(s_head_b, q + 1)
                dve.scalar_tensor_tensor(out=head_l[:, :, :], in0=head_b[:, :, :], scalar=SLOPE, in1=head_b[:, :, :],
                                         op0=ALU.mult, op1=ALU.max).then_inc(s_head_l, 1)
                dve.wait_ge(s_head_l, q + 1)
                dve.tensor_reduce(score[:, bass.ds(q * PT, PT)], head_l[:, :, :], AX_X, ALU.add).then_inc(s_score, 1)

            def pair_step(q, slot, turn):
                word = word_of(dve, q)
                windows(q, slot, turn, 0, word)
                if not isinstance(q, int) or q > 0:
                    relu(2 * q - 1, 1)
                windows(q, slot, turn, 1, word)
                relu(2 * q, 0)
                if not isinstance(q, int) or q > 0:
                    scores(q - 1, 1 - slot)

            def moments(n, b, rows_of, waited):
                waited()
                dve.bn_stats(node_st[:, n, :], rows_of[:, :]).then_inc(s_node_st[n], 1)
                dve.wait_ge(s_node_st[n], b + 1)
                dve.sem_inc(s_passed, 1)
                dve.bn_aggr(node_m[:, n, 0:2], node_st[:, n, :]).then_inc(s_node_m[n], 1)

            def inverse(n, b):
                dve.wait_ge(s_node_sd[n], b + 1)
                dve.reciprocal(node_m[:, n, 3:4], node_m[:, n, 2:3]).then_inc(s_node_inv[n], 1)
                dve.wait_ge(s_node_inv[n], b + 1)

            def node_step(i, u):
                if u == 0 and valid(i - 1):
                    b = i - 1
                    inverse(0, b)
                    wait(dve, s_node_o, b)
                    dve.tensor_scalar(node_t[:, :], node_y[:, :], node_m[:, 0, 0:1], node_m[:, 0, 3:4], ALU.subtract,
                                      ALU.mult).then_inc(s_node_t, 1)
                    dve.wait_ge(s_node_t, 4 * b + 1)
                    dve.tensor_tensor(node_t[:, :], node_t[:, :], gamma_row[:, :], ALU.mult).then_inc(s_node_t, 1)
                    dve.wait_ge(s_node_t, 4 * b + 2)
                    dve.tensor_tensor(node_t[:, :], node_t[:, :], beta_row[:, :], ALU.add).then_inc(s_node_t, 1)
                    dve.wait_ge(s_node_t, 4 * b + 3)
                    dve.wait_ge(s_node_r, 16 * (b + 1))
                    dve.tensor_tensor(node_t[:, :], node_t[:, :], node_r[:, :], ALU.add).then_inc(s_node_t, 1)
                    moments(1, b, node_t, lambda: dve.wait_ge(s_node_t, 4 * b + 4))
                if u == 1 and valid(i - 1):
                    b = i - 1
                    inverse(1, b)
                    wait(dve, s_node_out, 16 * b)
                    dve.tensor_scalar(node_o[:, :], node_t[:, :], node_m[:, 1, 0:1], node_m[:, 1, 3:4], ALU.subtract,
                                      ALU.mult).then_inc(s_node_o, 1)
                if u == 1 and valid(i):
                    if isinstance(i, int) and i == 0:
                        dve.wait_ge(s_late, 16 * NODE_WEIGHTS)
                    dve.wait_ge(s_node_h, i + 1)
                    wait(dve, s_node_y_out, 16 * i)
                    dve.tensor_tensor(node_y[:, :], wide[0][:, 0:P], bn_row[:, :], ALU.add).then_inc(s_node_y, 1)
                    moments(0, i, node_y, lambda: dve.wait_ge(s_node_y, i + 1))

            over_pairs(dve, pairs, blocks, pair_step, node_step)
            relu(groups - 1, 1)
            scores(pairs - 1, (pairs - 1) % 2)

            dve.wait_ge(s_score, pairs)
            full = n_edges // P
            if n_edges % P:
                dve.tensor_scalar(cols[:, 4:5], iota_f[:, 0:1], float(n_edges % P), -0.5, ALU.is_lt,
                                  ALU.add).then_inc(s_cast, 1)
                dve.wait_ge(s_cast, 6)
                dve.tensor_scalar(cols[:, 4:5], cols[:, 4:5], 3e38, None, ALU.mult).then_inc(s_cast, 1)
                dve.wait_ge(s_cast, 7)
                dve.tensor_scalar(cols[:, 4:5], cols[:, 4:5], 2.0, None, ALU.mult).then_inc(s_cast, 1)
                dve.wait_ge(s_cast, 8)
                dve.tensor_tensor(score[:, full:full + 1], score[:, full:full + 1], cols[:, 4:5],
                                  ALU.min).then_inc(s_soft, 1)
                full += 1
            else:
                dve.memset(cols[:, 4:5], 0.0).then_inc(s_soft, 1)
            if full < tiles:
                dve.memset(score[:, full:tiles], -3e38).then_inc(s_cast, 1)
                dve.wait_ge(s_cast, 9 if n_edges % P else 6)
            dve.wait_ge(s_soft, 1)
            dve.tensor_reduce(cols[:, 0:1], score[:, :], AX_X, ALU.max).then_inc(s_soft, 1)
            dve.wait_ge(s_max, 1)
            dve.tensor_scalar(cols[:, 2:3], cols[:, 1:2], -1.0 / H, None, ALU.mult).then_inc(s_soft, 1)
            dve.wait_ge(s_exp, 1)
            dve.tensor_scalar(nonzero[:, :], score[:, :], 0.0, None, ALU.not_equal).then_inc(s_soft, 1)
            dve.wait_ge(s_total, 1)
            dve.reciprocal(cols[:, 5:6], pre[0][:, 0:1]).then_inc(s_soft, 1)
            dve.wait_ge(s_counts, 1)
            dve.wait_ge(s_const, 9)
            kp = key_parts
            dve.tensor_scalar(flag[0:kp, :], pre[1][0:kp, 0:key_cols], 0.0, None, ALU.is_gt).then_inc(s_counts, 1)
            dve.tensor_scalar(key[0:kp, :], row_i[0:kp, 0:key_cols], float(-kp), KEY, ALU.mult, ALU.add).then_inc(
                s_counts, 1)
            dve.wait_ge(s_counts, 3)
            dve.tensor_reduce(cols[:, 6:7], flag[:, :], AX_X, ALU.add).then_inc(s_counts, 1)
            dve.tensor_scalar(key[0:kp, :], key[0:kp, :], iota_f[0:kp, 0:1], None, ALU.subtract).then_inc(s_seg_key, 1)
            dve.wait_ge(s_seg_key, 1)
            dve.tensor_tensor(key[:, :], key[:, :], flag[:, :], ALU.mult).then_inc(s_seg_key, 1)
            dve.wait_ge(s_counts, 5)
            dve.tensor_copy(count_i[:, :], cols[0:1, 7:8]).then_inc(s_left, 1)
            dve.wait_ge(s_left, 1)
            dve.wait_ge(s_seg_key, 2)
            left = dve.value_load(count_i[0:1, 0:1], min_val=1, max_val=tiles)

            with dve.Fori(0, left) as i:
                dve.tensor_reduce(cols[:, 8:9], key[:, :], AX_X, ALU.max).then_inc(s_seg_key, 1)
                dve.wait_ge(s_seg_max, i + 1)
                dve.tensor_scalar(tile_i[:, :], cols[0:1, 9:10], -1.0, KEY, ALU.mult, ALU.add).then_inc(s_seg_tile, 1)
                dve.scalar_tensor_tensor(out=key[:, :], in0=key[:, :], scalar=cols[:, 9:10], in1=key[:, :],
                                         op0=ALU.not_equal, op1=ALU.mult).then_inc(s_seg_key, 1)
                dve.wait_ge(s_seg_tile, i + 1)
                dve.sem_inc(s_passed, 1)
                t = dve.value_load(tile_i[0:1, 0:1], min_val=0, max_val=tiles - 1)
                dve.tensor_scalar(seg_f[:, 0:1], score[:, bass.ds(t, 1)], cols[:, 5:6], None, ALU.mult).then_inc(
                    s_seg, 1)
                dve.wait_ge(s_seg_in, 48 * i + 48)
                dve.tensor_copy(seg_f[:, 1:2], seg_col[:, 0:1]).then_inc(s_seg, 1)
                dve.wait_ge(s_seg, 10 * i + 2)
                dve.tensor_scalar(seg_w[:, :], seg_row[:, :], seg_f[:, 1:2], seg_f[:, 0:1], ALU.is_equal,
                                  ALU.mult).then_inc(s_seg, 1)
                dve.wait_ge(s_seg_mm, 2 * i + 1)
                dve.tensor_copy(seg_t[:, :], pre[0][:, 0:P]).then_inc(s_seg, 1)
                dve.scalar_tensor_tensor(out=seg_s[:, :], in0=seg_row[:, :], scalar=seg_f[:, 1:2], in1=before[:, :],
                                         op0=ALU.is_equal, op1=ALU.mult).then_inc(s_seg, 1)
                dve.wait_ge(s_seg, 10 * i + 5)
                dve.tensor_reduce(seg_f[:, 2:3], seg_s[:, :], AX_X, ALU.max).then_inc(s_seg, 1)
                dve.tensor_tensor(seg_f[:, 3:4], iota_f[:, 0:1], seg_f[:, 1:2], ALU.subtract).then_inc(s_seg, 1)
                dve.wait_ge(s_seg, 10 * i + 7)
                dve.tensor_scalar(seg_f[:, 4:5], seg_f[:, 3:4], float(n_pad), seg_f[:, 2:3], ALU.add,
                                  ALU.mult).then_inc(s_seg, 1)
                dve.wait_ge(s_seg, 10 * i + 8)
                dve.tensor_tensor(seg_to[:, :], seg_f[:, 4:5], seg_f[:, 1:2], ALU.add).then_inc(s_seg, 1)
                dve.wait_ge(s_seg_mm, 2 * i + 2)
                dve.tensor_copy(seg_o[:, :], pre[0][:, P:2 * P]).then_inc(s_seg, 1)
                dve.wait_ge(s_seg_add, 16 * i + 16)
                dve.wait_ge(s_seg_y, 32 * i + 32)
                for n, v in enumerate((seg_y, seg_x)):
                    at = 11 * i + 7 * n
                    dve.bn_stats(seg_st[:, n, :], v[:, :]).then_inc(s_seg_ln, 1)
                    dve.wait_ge(s_seg_ln, at + 1)
                    dve.sem_inc(s_passed, 1)
                    dve.bn_aggr(seg_m[:, n, 0:2], seg_st[:, n, :]).then_inc(s_seg_ln, 1)
                    dve.wait_ge(s_seg_sd, 2 * i + n + 1)
                    dve.reciprocal(seg_m[:, n, 3:4], seg_m[:, n, 2:3]).then_inc(s_seg_ln, 1)
                    dve.wait_ge(s_seg_ln, at + 3)
                    dve.tensor_scalar((seg_x if n == 0 else seg_o)[:, :], v[:, :], seg_m[:, n, 0:1], seg_m[:, n, 3:4],
                                      ALU.subtract, ALU.mult).then_inc(s_seg_ln, 1)
                    if n == 0:
                        dve.wait_ge(s_seg_ln, at + 4)
                        dve.tensor_tensor(seg_x[:, :], seg_x[:, :], gamma_row[:, :], ALU.mult).then_inc(s_seg_ln, 1)
                        dve.wait_ge(s_seg_ln, at + 5)
                        dve.tensor_tensor(seg_x[:, :], seg_x[:, :], beta_row[:, :], ALU.add).then_inc(s_seg_ln, 1)
                        dve.wait_ge(s_seg_ln, at + 6)
                        dve.tensor_tensor(seg_x[:, :], seg_x[:, :], seg_xs[:, :], ALU.add).then_inc(s_seg_ln, 1)
                        dve.wait_ge(s_seg_ln, at + 7)
                dve.wait_ge(s_seg_out, 16 * i + 16)


_ROWS = ("x_rows", "x_blocks", "x_strided", "edges", "src_pairs", "dst_pairs", "src_tiles", "dst_tiles", "wqT", "wkT",
         "weT", "wv", "wn", "bn", "bq", "bk", "bv", "be", "A1", "b1", "A2", "b2", "gamma", "beta")


def lay_out(x, src, dst, edge_attr_64, **w):
    x, src, dst, edge_attr = (np.asarray(a) for a in (x, src, dst, edge_attr_64))
    w = {k.replace("L0_gnn_", ""): np.asarray(v) for k, v in w.items()}
    n, d = x.shape
    e, de = edge_attr.shape
    step = P * CHUNK
    chunks = -(-n // step)
    chunks += chunks % 2
    pairs = -(-e // PAIR)
    pairs += 1 - pairs % 2
    xp = np.pad(x, ((0, chunks * step - n), (0, 0)))
    ep = np.pad(edge_attr, ((0, pairs * PAIR - e), (0, 0)))
    sp, dp = (np.pad(a, (0, pairs * PAIR - e), mode="edge") for a in (src, dst))
    arrays = {
        "x_rows": xp,
        "x_blocks": xp.reshape(chunks * CHUNK, P, d).transpose(0, 2, 1),
        "x_strided": xp.reshape(P, chunks, CHUNK, d).transpose(1, 3, 2, 0).reshape(chunks, d, step),
        "edges": ep.reshape(pairs, 2, GROUP, de).transpose(0, 1, 3, 2).reshape(pairs, 2 * de, GROUP),
        "src_pairs": sp.reshape(pairs, PT, P).transpose(0, 2, 1),
        "dst_pairs": dp.reshape(pairs, PAIR),
        "src_tiles": sp.reshape(pairs * PT, P),
        "dst_tiles": dp.reshape(pairs * PT, P),
        "wqT": w["Wq"].T, "wkT": w["Wk"].T, "weT": w["We"].T, "wv": w["Wv"], "wn": w["Wn"],
        "bn": w["bn"], "bq": w["bq"], "bk": w["bk"], "bv": w["bv"], "be": w["be"], "A1": w["A1"], "b1": w["b1"],
        "A2": w["A2"], "b2": w["b2"], "gamma": w["gamma"], "beta": w["beta"],
    }
    return {k: np.ascontiguousarray(arrays[k]) for k in _ROWS}


def kernel(**inputs):
    import concourse.bacc as bacc
    from concourse.bass_utils import run_bass_kernel_spmd

    n, d = inputs["x"].shape
    arrays = {f"in_{k}_dram": a for k, a in lay_out(**inputs).items()}
    nc = bacc.Bacc("TRN2", target_bir_lowering=False, num_devices=1)
    args = [nc.dram_tensor(k, a.shape, mybir.dt.from_np(a.dtype), kind="ExternalInput").ap() for k, a in arrays.items()]
    out = nc.dram_tensor("out_0_dram", (arrays["in_x_rows_dram"].shape[0] + OUT_MORE, d), F32, kind="ExternalOutput").ap()
    build(nc, *args, out, inputs["edge_attr_64"].shape[0])
    r = run_bass_kernel_spmd(nc, [arrays], core_ids=[0])
    return r.results[0]["out_0_dram"][:n]
```

```python
from contextlib import ExitStack

import numpy as np
import concourse.bass as bass
from concourse import mybir

F32 = mybir.dt.float32
BF16 = mybir.dt.bfloat16
I32 = mybir.dt.int32
ALU = mybir.AluOpType
ACT = mybir.ActivationFunctionType
AX_X = mybir.AxisListType.X
RED = bass.bass_isa.ReduceOp

P = 128
GROUP = 512
TILES = GROUP // P
PAIR = 2 * GROUP
PT = PAIR // P
CHUNK = 4
WIDE = 3
EXTRA = 1
SLOPE = 0.2
EPS = 1e-5
MORE = 256
KEY = 8192.0
OUT_MORE = P
BLOCK_LAG = 3
XA = 6


def largest_divisor(n, most):
    return max(d for d in range(1, most + 1) if n % d == 0)


def roll(eng, total, peel, ring, step, tail=0):
    for n in range(peel):
        step(n, n % ring, n // ring)
    turns, rest = divmod(total - peel - tail, ring)
    assert turns >= 0 and rest == 0
    if turns:
        with eng.Fori(0, turns) as i:
            for u in range(ring):
                n = peel + u
                step(n + ring * i, n % ring, n // ring + i)
    for n in range(total - tail, total):
        step(n, n % ring, n // ring)


def over_pairs(eng, pairs, blocks, pair_step, node_step):
    for q in range(3):
        pair_step(q, q % 2, q // 2)
    total = (pairs - 3) // 2
    with_nodes = blocks + BLOCK_LAG
    assert (pairs - 3) % 2 == 0 and total > with_nodes + 1

    def iteration(i, nodes):
        for u in range(2):
            pair_step(3 + u + 2 * i, (3 + u) % 2, (3 + u) // 2 + i)
            if nodes:
                node_step(i, u)

    for i in range(BLOCK_LAG):
        iteration(i, True)
    with eng.Fori(BLOCK_LAG, blocks) as i:
        iteration(i, True)
    for i in range(blocks, with_nodes):
        iteration(i, True)
    with eng.Fori(with_nodes, total - 1) as i:
        iteration(i, False)
    iteration(total - 1, False)


def wait(eng, sem, value):
    if not isinstance(value, int) or value > 0:
        eng.wait_ge(sem, value)


def build(nc, x_rows, x_blocks, edges, src_pairs, dst_pairs, src_tiles, dst_tiles, wqT, wkT, weT, wv, wn,
          bn, bq, bk, bv, be, A1, b1, A2, b2, gamma, beta, out, n_edges):
    n_pad, D = x_rows.shape
    H = A2.shape[1]
    DE = weT.shape[1]
    pairs = edges.shape[0]
    groups = 2 * pairs
    tiles = PT * pairs
    blocks = n_pad // P
    chunks = blocks // CHUNK
    CW = CHUNK * P
    assert chunks * CW == n_pad and D == P and 2 * DE == P and tiles < KEY and blocks <= MORE
    info_parts = largest_divisor(groups, P)
    info_cols = groups // info_parts
    table_peel = XA + 1 + (chunks - XA - 1) % XA
    span_peel = max(table_peel, info_cols)
    span_peel += (chunks - span_peel) % XA
    assert span_peel <= chunks - XA
    key_parts = largest_divisor(tiles, P)
    key_cols = tiles // key_parts

    pq_dram = nc.dram_tensor("pq_dram", (n_pad, D), F32).ap()
    y_dram = nc.dram_tensor("y_dram", (n_pad + P, D), F32).ap()
    span_dram = nc.dram_tensor("span_dram", (groups, 2), I32).ap()

    with ExitStack() as ctx:
        def sb(name, shape, dt):
            return ctx.enter_context(nc.sbuf_tensor(name, shape, dt))

        def ps(name, shape, dt):
            return ctx.enter_context(nc.psum_tensor(name, shape, dt))

        def sem(name):
            return ctx.enter_context(nc.semaphore(name))

        pk = sb("pk", [P, blocks + EXTRA, 3, P], BF16)
        xa = sb("xa", [P, XA, CW], F32)
        stage = sb("stage", [P, XA, CW], F32)
        pk_rest = sb("pk_rest", [P, WIDE, CW], F32)
        w_in = sb("w_in", [P, 2, P], F32)
        we_in = sb("we_in", [P, 2, P], F32)
        a1_in = sb("a1_in", [P, 3, P], F32)
        wv_sb = sb("wv_sb", [P, P], F32)
        wn_sb = sb("wn_sb", [P, P], F32)
        a2_sb = sb("a2_sb", [P, H], F32)
        bcols = sb("bcols", [P, 4], F32)
        b2_row = sb("b2_row", [P, H], F32)
        bv_row = sb("bv_row", [P, P], F32)
        bn_row = sb("bn_row", [P, P], F32)
        gamma_row = sb("gamma_row", [P, P], F32)
        beta_row = sb("beta_row", [P, P], F32)
        w_fold = sb("w_fold", [P, 4, P], F32)
        bias_col = sb("bias_col", [P, 2], F32)
        iota_i = sb("iota_i", [P, P], I32)
        iota_f = sb("iota_f", [P, P], F32)
        row_i = sb("row_i", [P, P], I32)
        ident = sb("ident", [P, P], F32)
        before = sb("before", [P, P], F32)
        ones_f = sb("ones_f", [P, P], F32)
        ones_b = sb("ones_b", [P, 1], BF16)
        spans = sb("spans", [info_parts, 8, info_cols], I32)
        span_row = sb("span_row", [1, groups, 2], I32)
        rounds_f = sb("rounds_f", [1, groups], F32)
        sums_f = sb("sums_f", [1, groups], F32)
        zeros_f = sb("zeros_f", [1, groups], F32)
        info = sb("info", [1, groups, 4], I32)
        edge = sb("edge", [P, 2, GROUP], F32)
        dst_b = sb("dst_b", [P, 2, PAIR], I32)
        src_i = sb("src_i", [P, 2, PT], I32)
        rows = sb("rows", [P, 4, TILES, P], F32)
        onehot = sb("onehot", [P, 2, GROUP], BF16)
        extra = sb("extra", [P, EXTRA, GROUP], BF16)
        sloped = sb("sloped", [P, 2, GROUP], F32)
        hidden = sb("hidden", [P, 2, GROUP], F32)
        head_b = sb("head_b", [P, PT, H], F32)
        head_l = sb("head_l", [P, PT, H], F32)
        score = sb("score", [P, tiles + 1], F32)
        cols = sb("cols", [P, 16], F32)
        nonzero = sb("nonzero", [P, tiles], BF16)
        key = sb("key", [P, key_cols], F32)
        flag = sb("flag", [P, key_cols], F32)
        count_i = sb("count_i", [1, 1], I32)
        tile_i = sb("tile_i", [1, 1], I32)
        seg_row = sb("seg_row", [P, P], I32)
        seg_col = sb("seg_col", [P, 2], I32)
        seg_f = sb("seg_f", [P, 8], F32)
        seg_to = sb("seg_to", [P, 1], I32)
        seg_x = sb("seg_x", [P, P], F32)
        seg_w = sb("seg_w", [P, P], F32)
        seg_s = sb("seg_s", [P, P], F32)
        seg_t = sb("seg_t", [P, P], F32)
        seg_o = sb("seg_o", [P, P], F32)
        seg_y = sb("seg_y", [P, P], F32)
        seg_xs = sb("seg_xs", [P, P], F32)
        seg_st = sb("seg_st", [P, 2, 6], F32)
        seg_m = sb("seg_m", [P, 2, 4], F32)
        node_x = sb("node_x", [P, P], F32)
        node_r = sb("node_r", [P, P], F32)
        node_y = sb("node_y", [P, P], F32)
        node_t = sb("node_t", [P, P], F32)
        node_o = sb("node_o", [P, P], F32)
        node_st = sb("node_st", [P, 2, 6], F32)
        node_m = sb("node_m", [P, 2, 4], F32)
        pk_words = pk[:, :, :, :].rearrange("p b c n -> p (b c n)").bitcast(F32)
        span_at = (blocks + EXTRA) * 3 * P // 2 - info_cols * GROUP
        assert (info_cols + 3) * CHUNK * 3 * P // 2 <= span_at
        span_in = pk_words[0:info_parts, span_at:span_at + info_cols * GROUP].bitcast(I32)

        wide_all = ps("wide", [P, WIDE, 2, 512], F32)
        wide = [wide_all[:, i, :, :].rearrange("p b n -> p (b n)") for i in range(WIDE)]
        pre = [wide_all[:, WIDE - 1, i, :] for i in range(2)]
        heads = [ps(f"heads{i}", [P, 512], F32) for i in range(2)]

        s_weights = sem("weights_loaded")
        s_passed = sem("passed")
        s_const = sem("constants_made")
        s_bias_col = sem("bias_column_ready")
        s_fold = sem("weights_folded")
        s_folded = sem("folded_copied")
        s_iota = sem("iota_made")
        s_cast = sem("constants_cast")
        s_span_in = sem("dst_for_spans_loaded")
        s_span = sem("span_steps")
        s_span_out = sem("spans_stored")
        s_span_row = sem("spans_back")
        s_info = sem("info_steps")
        s_xa = [sem(f"nodes_loaded{i}") for i in range(XA)]
        s_table = sem("table_products")
        s_pq_stage = sem("pq_staged")
        s_pq_out = [sem(f"pq_stored{i}") for i in range(XA)]
        s_pk_hi = sem("pk_high_made")
        s_pk_rest = sem("pk_rest_made")
        s_pk_mid = sem("pk_mid_made")
        s_pk_lo = sem("pk_low_made")
        s_first = sem("first_weights_loaded")
        s_bias = sem("biases_loaded")
        s_late = sem("node_weights_loaded")
        s_y_init = sem("rows_behind_y_written")
        s_edge = [sem(f"edges_loaded{i}") for i in range(2)]
        s_dst = [sem(f"dst_loaded{i}") for i in range(2)]
        s_src = [sem(f"src_loaded{i}") for i in range(2)]
        s_rows = [sem(f"rows_gathered{i}") for i in range(4)]
        s_edge_used = sem("edges_used")
        s_onehot = sem("onehot_ready")
        s_extra = sem("extra_onehots_ready")
        s_extra_used = sem("extra_onehots_used")
        s_pre = sem("pre_ready")
        s_sloped = sem("sloped_ready")
        s_hidden = sem("hidden_ready")
        s_heads = sem("heads_ready")
        s_head_b = sem("heads_biased")
        s_head_l = sem("heads_relued")
        s_score = sem("scores_ready")
        s_soft = sem("softmax_steps")
        s_max_part = sem("part_of_maximum_ready")
        s_max = sem("maximum_ready")
        s_exp = sem("exponentials_ready")
        s_total = sem("total_ready")
        s_counts = sem("tile_counts_ready")
        s_left = sem("tiles_counted")
        s_seg_key = sem("segment_key_steps")
        s_seg_max = sem("segment_key_reduced")
        s_seg_tile = sem("segment_tile_known")
        s_seg_dst = sem("segment_dst_loaded")
        s_seg_src = sem("segment_src_loaded")
        s_seg_row = sem("segment_src_row_loaded")
        s_seg_x = sem("segment_rows_gathered")
        s_seg = sem("segment_steps")
        s_seg_mm = sem("segment_products")
        s_seg_y = sem("segment_y_gathered")
        s_seg_xs = sem("segment_own_rows_gathered")
        s_seg_y_out = sem("segment_y_stored")
        s_seg_ln = sem("segment_norm_steps")
        s_seg_sd = sem("segment_deviations")
        s_seg_out = sem("segment_rows_stored")
        s_node_x = sem("node_columns_loaded")
        s_node_r = sem("node_rows_loaded")
        s_node_h = sem("node_products")
        s_node_y = sem("node_y_ready")
        s_node_y_out = sem("node_y_stored")
        s_node_st = [sem(f"node_stats{n}") for n in range(2)]
        s_node_m = [sem(f"node_moments{n}") for n in range(2)]
        s_node_sd = [sem(f"node_deviations{n}") for n in range(2)]
        s_node_inv = [sem(f"node_inverse_deviations{n}") for n in range(2)]
        s_node_t = sem("node_first_norm_steps")
        s_node_o = sem("node_result_ready")
        s_node_out = sem("node_result_stored")

        pq_blocks = pq_dram.rearrange("(b p) d -> p b d", p=P)
        y_blocks = y_dram.rearrange("(b p) d -> b p d", p=P)
        out_blocks = out.rearrange("(b p) d -> b p d", p=P)
        x_row_blocks = x_rows.rearrange("(b p) d -> b p d", p=P)
        EDGE_WEIGHTS, NODE_WEIGHTS = 4, 6

        def valid(b):
            return not isinstance(b, int) or 0 <= b < blocks

        def info_of(eng, g, n, most):
            return eng.value_load(info[0:1, bass.ds(g, 1), n:n + 1].rearrange("a b c -> a (b c)"), min_val=0,
                                  max_val=most)

        def word_of(eng, g):
            return info_of(eng, g, 3, 4 * MORE * MORE - 1)

        def window_of(word, n):
            part = word & (2 * MORE - 1) if n == 0 else word >> (2 * MORE).bit_length() - 1
            return (part & (MORE - 1)).with_bounds(min_val=0, max_val=blocks - 1), part >> MORE.bit_length() - 1

        def rounds_of(eng, g):
            return info_of(eng, g, 1, blocks // EXTRA + 1), info_of(eng, g, 2, groups * (blocks // EXTRA + 1))

        def row_of(eng, t, b, s):
            eng.dma_start(t[:, :], b.rearrange("(a n) -> a n", a=1).to_broadcast([P, b.shape[0]])).then_inc(s, 16)

        SPAN_STEPS = 2 * info_cols + 5
        halves = (0, tiles // 2), (tiles // 2, tiles)
        MADE = 9

        block = ctx.enter_context(nc.Block())

        @block.sync
        def _(sp):
            sp.dma_start(w_in[:, 0, :], wqT).then_inc(s_first, 16)
            sp.dma_start(a1_in[:, :, :], A1.rearrange("(c p) n -> p c n", p=P)).then_inc(s_first, 16)

            def pq_store(c, slot):
                wait(sp, s_pq_stage, c + 1)
                sp.dma_start(pq_blocks[:, bass.ds(c * CHUNK, CHUNK), :],
                             stage[:, slot, :].rearrange("p (j d) -> p j d", j=CHUNK)).then_inc(s_pq_out[slot], 16)

            def table_step(c, slot, turn):
                wait(sp, s_table, c - XA + 1)
                sp.dma_start(xa[:, slot, :].rearrange("p (j n) -> p j n", j=CHUNK),
                             x_blocks[bass.ds(c * CHUNK, CHUNK), :, :].rearrange("j p n -> p j n")).then_inc(
                    s_xa[slot], 16)
                if isinstance(c, int) and c == 1:
                    sp.dma_start(span_in, dst_pairs.rearrange("a n -> (a n)").rearrange(
                        "(p m) -> p m", p=info_parts)).then_inc(s_span_in, 16)
                if isinstance(c, int) and c == XA - 1:
                    for n, b in enumerate((bq, bk, be, b1)):
                        sp.dma_start(bcols[:, n:n + 1], b.rearrange("(p a) -> p a", a=1)).then_inc(s_bias, 16)
                    sp.dma_start(we_in[:, 0, 0:DE], weT).then_inc(s_weights, 16)
                    sp.dma_start(we_in[:, 1, DE:P], weT).then_inc(s_weights, 16)
                    sp.dma_start(a2_sb[:, :], A2).then_inc(s_weights, 16)
                    row_of(sp, b2_row, b2, s_weights)
                if not isinstance(c, int) or c > XA:
                    pq_store(c - XA - 1, (slot - 1) % XA)
                if isinstance(c, int) and c == chunks - XA:
                    sp.wait_ge(s_span, SPAN_STEPS)
                    sp.dma_start(span_dram.rearrange("(p g) c -> p (g c)", p=info_parts),
                                 spans[:, 6:8, :].rearrange("p a b -> p (a b)")).then_inc(s_span_out, 16)
                if isinstance(c, int) and c == chunks - XA + 2:
                    sp.wait_ge(s_span_out, 16)
                    sp.dma_start(span_row[:, :, :], span_dram.rearrange("(a g) c -> a g c", a=1)).then_inc(
                        s_span_row, 16)

            roll(sp, chunks, table_peel, XA, table_step, tail=XA)

            def pair_step(q, slot, turn):
                wait(sp, s_hidden, 2 * q - 3)
                sp.dma_start(dst_b[:, slot, :],
                             dst_pairs[bass.ds(q, 1), :].to_broadcast([P, PAIR])).then_inc(s_dst[slot], 16)
                wait(sp, s_edge_used, q - 1)
                sp.dma_start(edge[:, slot, :], edges[bass.ds(q, 1), :, :].rearrange("a p n -> (a p) n")).then_inc(
                    s_edge[slot], 16)
                for h in range(2):
                    wait(sp, s_rows[2 * slot + h], 64 * turn)
                sp.dma_start(src_i[:, slot, :], src_pairs[bass.ds(q, 1), :, :].rearrange("a p n -> (a p) n")).then_inc(
                    s_src[slot], 16)

            pair_step(0, 0, 0)
            pair_step(1, 1, 0)

            for c in range(chunks - XA - 1, chunks):
                pq_store(c, c % XA)

            def node_step(i, u):
                if u == 1 and valid(i):
                    wait(sp, s_node_h, i)
                    sp.dma_start(node_x[:, :], x_blocks[bass.ds(i, 1), :, :].rearrange("a p n -> (a p) n")).then_inc(
                        s_node_x, 16)
                if u == 1 and valid(i - 1):
                    wait(sp, s_node_t, 4 * (i - 1))
                    sp.dma_start(node_r[:, :],
                                 x_row_blocks[bass.ds(i - 1, 1), :, :].rearrange("a p n -> (a p) n")).then_inc(
                        s_node_r, 16)
                if u == 0 and valid(i - 2):
                    wait(sp, s_node_y, i - 1)
                    sp.dma_start(y_blocks[bass.ds(i - 2, 1), :, :].rearrange("a p n -> (a p) n"),
                                 node_y[:, :]).then_inc(s_node_y_out, 16)
                if u == 0 and valid(i - 3):
                    wait(sp, s_node_o, i - 2)
                    sp.dma_start(out_blocks[bass.ds(i - 3, 1), :, :].rearrange("a p n -> (a p) n"),
                                 node_o[:, :]).then_inc(s_node_out, 16)

            over_pairs(sp, pairs, blocks, lambda q, slot, turn: None if isinstance(q, int) and q < 2 else
                       pair_step(q, slot, turn), node_step)

            sp.wait_ge(s_left, 1)
            left = sp.value_load(count_i[0:1, 0:1], min_val=1, max_val=tiles)
            with sp.Fori(0, left) as i:
                sp.wait_ge(s_seg_tile, i + 1)
                sp.sem_inc(s_passed, 1)
                t = sp.value_load(tile_i[0:1, 0:1], min_val=0, max_val=tiles - 1)
                with nc.allow_non_contiguous_dma(reason="one index per partition"):
                    sp.dma_start(seg_col[:, 1:2], dst_tiles[bass.ds(t, 1), :].rearrange("a p -> p a")).then_inc(
                        s_seg_dst, 16)
                    sp.dma_start(seg_col[:, 0:1], src_tiles[bass.ds(t, 1), :].rearrange("a p -> p a")).then_inc(
                        s_seg_src, 16)
                sp.dma_start(seg_row[:, :], src_tiles[bass.ds(t, 1), :].to_broadcast([P, P])).then_inc(s_seg_row, 16)

            sp.wait_ge(s_node_out, 16 * blocks)
            sp.wait_ge(s_seg_out, 16 * left)
            sp.sem_inc(s_passed, 1)

        @block.gpsimd
        def _(pool):
            pool.iota(iota_i[:, :], [[P, P]], base=0, channel_multiplier=1).then_inc(s_iota, 1)
            pool.iota(row_i[:, :], [[1, P]], base=0, channel_multiplier=0).then_inc(s_iota, 1)
            pool.memset(ones_f[:, :], 1.0).then_inc(s_const, 1)
            pool.memset(ident[:, :], 0.0).then_inc(s_const, 1)
            pool.memset(ones_b[:, :], 1.0).then_inc(s_const, 1)
            pool.memset(zeros_f[:, :], 0.0).then_inc(s_const, 1)
            pool.memset(info[:, :, :], 0).then_inc(s_const, 1)
            pool.wait_ge(s_const, 5)
            pool.affine_select(out=ident[:, :], in_=ident[:, :], compare_op=ALU.not_equal, fill=1.0, base=0,
                               pattern=[[-1, P]], channel_multiplier=1).then_inc(s_const, 1)
            pool.affine_select(out=before[:, :], in_=ones_f[:, :], compare_op=ALU.is_gt, fill=0.0, base=0,
                               pattern=[[-1, P]], channel_multiplier=1).then_inc(s_const, 1)
            pool.memset(key[:, :], 0.0).then_inc(s_const, 1)
            pool.memset(flag[:, :], 0.0).then_inc(s_const, 1)

            def table_step(c, slot, turn):
                pool.wait_ge(s_pk_mid, c + 1)
                blocks_of = bass.ds(c * CHUNK, CHUNK)
                pool.tensor_tensor(pk[:, blocks_of, 2, :], pk_rest[:, slot % WIDE, :].rearrange("p (j d) -> p j d", j=CHUNK),
                                   pk[:, blocks_of, 1, :], ALU.subtract).then_inc(s_pk_lo, 1)

            roll(pool, chunks, table_peel, XA, table_step)

            for slot in range(XA):
                pool.wait_ge(s_pq_out[slot], 16 * len(range(slot, chunks, XA)))

            def pair_step(q, slot, turn):
                for h in range(2):
                    if h == 0:
                        pool.wait_ge(s_src[slot], 16 * (turn + 1))
                    wait(pool, s_pre, 2 * q + h - 3)
                    pool.sem_inc(s_passed, 1)
                    for k in range(TILES):
                        pool.indirect_dma_start(
                            rows[:, 2 * slot + h, k, :], None, pq_dram,
                            bass.IndirectOffsetOnAxis(src_i[:, slot, h * TILES + k:h * TILES + k + 1], 0),
                        ).then_inc(s_rows[2 * slot + h], 16)

            roll(pool, pairs, 3, 2, pair_step)

            pool.wait_ge(s_soft, 2)
            pool.partition_all_reduce(cols[:, 1:2], cols[:, 0:1], P, RED.max).then_inc(s_max, 1)
            pool.wait_ge(s_counts, 4)
            pool.partition_all_reduce(cols[:, 7:8], cols[:, 6:7], P, RED.add).then_inc(s_counts, 1)

            pool.wait_ge(s_left, 1)
            pool.wait_ge(s_y_init, 16)
            pool.wait_ge(s_node_y_out, 16 * blocks)
            pool.wait_ge(s_node_out, 16 * blocks)
            left = pool.value_load(count_i[0:1, 0:1], min_val=1, max_val=tiles)
            with pool.Fori(0, left) as i:
                pool.wait_ge(s_seg_key, 2 * i + 3)
                pool.sem_inc(s_passed, 1)
                pool.partition_all_reduce(cols[:, 9:10], cols[:, 8:9], P, RED.max).then_inc(s_seg_max, 1)
                pool.wait_ge(s_seg_dst, 16 * i + 16)
                pool.sem_inc(s_passed, 1)
                pool.indirect_dma_start(seg_x[:, :], None, x_rows,
                                        bass.IndirectOffsetOnAxis(seg_col[:, 1:2], 0)).then_inc(s_seg_x, 16)
                pool.wait_ge(s_seg_src, 16 * i + 16)
                pool.sem_inc(s_passed, 1)
                pool.indirect_dma_start(seg_y[:, :], None, y_dram,
                                        bass.IndirectOffsetOnAxis(seg_col[:, 0:1], 0)).then_inc(s_seg_y, 16)
                pool.indirect_dma_start(seg_xs[:, :], None, x_rows,
                                        bass.IndirectOffsetOnAxis(seg_col[:, 0:1], 0)).then_inc(s_seg_xs, 16)
                pool.wait_ge(s_seg, 10 * i + 10)
                pool.sem_inc(s_passed, 1)
                pool.indirect_dma_start(y_dram, bass.IndirectOffsetOnAxis(seg_to[:, 0:1], 0), seg_y[:, :],
                                        None).then_inc(s_seg_y_out, 16)
                pool.wait_ge(s_seg_ln, 11 * i + 11)
                pool.sem_inc(s_passed, 1)
                pool.indirect_dma_start(out, bass.IndirectOffsetOnAxis(seg_to[:, 0:1], 0), seg_o[:, :],
                                        None).then_inc(s_seg_out, 16)
                pool.wait_ge(s_seg_y_out, 16 * i + 16)
                pool.wait_ge(s_seg_out, 16 * i + 16)

        @block.scalar
        def _(act):
            act.dma_start(w_in[:, 1, :], wkT).then_inc(s_first, 16)

            def middle(c, slot):
                act.wait_ge(s_pk_rest, c + 1)
                act.copy(pk[:, bass.ds(c * CHUNK, CHUNK), 1, :],
                         pk_rest[:, slot % WIDE, :].rearrange("p (j d) -> p j d", j=CHUNK)).then_inc(s_pk_mid, 1)

            def table_step(c, slot, turn):
                act.wait_ge(s_table, c + 1)
                both = wide[slot % WIDE][:, :].rearrange("p (j t d) -> p j t d", j=CHUNK, t=2)
                wait(act, s_pq_out[slot], 16 * turn)
                act.copy(stage[:, slot, :].rearrange("p (j d) -> p j d", j=CHUNK), both[:, :, 0, :]).then_inc(
                    s_pq_stage, 1)
                act.copy(pk[:, bass.ds(c * CHUNK, CHUNK), 0, :], both[:, :, 1, :]).then_inc(s_pk_hi, 1)
                if not isinstance(c, int) or c > 0:
                    middle(c - 1, (slot - 1) % XA)

            roll(act, chunks, table_peel, XA, table_step)
            middle(chunks - 1, chunks - 1)

            act.dma_start(wv_sb[:, :], wv).then_inc(s_late, 16)
            act.dma_start(wn_sb[:, :], wn).then_inc(s_late, 16)
            for t, b in ((bv_row, bv), (bn_row, bn), (gamma_row, gamma), (beta_row, beta)):
                row_of(act, t, b, s_late)

            act.wait_ge(s_bias_col, 1)
            act.wait_ge(s_late, 16 * NODE_WEIGHTS)
            act.dma_start(y_dram[n_pad:n_pad + P, :], bn_row[:, :]).then_inc(s_y_init, 16)

            def pair_step(q, slot, turn):
                for h in range(2):
                    act.wait_ge(s_pre, 2 * q + h + 1)
                    wait(act, s_hidden, 2 * q + h - 1)
                    act.activation(sloped[:, h, :], pre[h][:, :], ACT.Identity, bias=bias_col[:, 1:2],
                                   scale=SLOPE).then_inc(s_sloped, 1)

            def node_step(i, u):
                n, b = (1, i - 1) if u == 0 else (0, i)
                if valid(b):
                    act.wait_ge(s_node_m[n], b + 1)
                    act.activation(node_m[:, n, 2:3], node_m[:, n, 1:2], ACT.Sqrt, bias=cols[:, 12:13]).then_inc(
                        s_node_sd[n], 1)

            over_pairs(act, pairs, blocks, pair_step, node_step)

            act.wait_ge(s_soft, 3)
            for n, (a, b) in enumerate(halves):
                act.activation(score[:, a:b], score[:, a:b], ACT.Exp, bias=cols[:, 2:3], scale=1.0 / H,
                               accum_out=cols[:, 13 + n:14 + n]).then_inc(s_exp, 1)

            act.wait_ge(s_left, 1)
            left = act.value_load(count_i[0:1, 0:1], min_val=1, max_val=tiles)
            with act.Fori(0, left) as i:
                for n in range(2):
                    act.wait_ge(s_seg_ln, 11 * i + (2, 9)[n])
                    act.activation(seg_m[:, n, 2:3], seg_m[:, n, 1:2], ACT.Sqrt, bias=cols[:, 12:13]).then_inc(
                        s_seg_sd, 1)

        @block.tensor
        def _(pe):
            fold = heads[0][:, 0:4 * P].rearrange("p (c n) -> p c n", c=4)
            pe.wait_ge(s_first, 48)
            for n in range(2):
                last = pe.matmul(fold[:, n, :], w_in[:, n, :], a1_in[:, n, :], start=True, stop=True)
            last.then_inc(s_fold, 1)

            def table_step(c, slot, turn):
                pe.wait_ge(s_xa[slot], 16 * (turn + 1))
                if isinstance(c, int) and c == 0:
                    pe.wait_ge(s_folded, 1)
                wait(pe, s_pq_stage, c - WIDE + 1)
                wait(pe, s_pk_rest, c - WIDE + 1)
                for j in range(CHUNK):
                    last = pe.matmul(wide[slot % WIDE][:, 2 * j * P:2 * (j + 1) * P], xa[:, slot, j * P:(j + 1) * P],
                                     w_fold[:, 0:2, :].rearrange("p c n -> p (c n)"), start=True, stop=True)
                last.then_inc(s_table, 1)
                if isinstance(c, int) and c == XA:
                    pe.wait_ge(s_bias, 64)
                    for n in range(3):
                        pe.matmul(heads[1][:, 0:1], a1_in[:, n, :], bcols[:, n:n + 1], start=(n == 0), stop=(n == 2))
                    pe.wait_ge(s_weights, 16 * EDGE_WEIGHTS)
                    pe.wait_ge(s_cast, 2)
                    pe.matmul(fold[:, 2, :], we_in[:, 0, :], a1_in[:, 2, :], start=True, stop=True)
                    pe.matmul(fold[:, 3, :], we_in[:, 1, :], a1_in[:, 2, :], start=True, stop=True).then_inc(s_fold, 1)

            roll(pe, chunks, table_peel, XA, table_step)

            pe.wait_ge(s_pk_lo, chunks)
            pe.wait_ge(s_pk_hi, chunks)
            pe.wait_ge(s_pq_stage, chunks)
            pe.wait_ge(s_folded, 3)
            pe.wait_ge(s_info, 8)
            pe.sem_inc(s_extra_used, 1)
            flat = pk[:, :, :, :].rearrange("p b c n -> p (b c n)")

            def score_mm(h, slot):
                for k in range(TILES):
                    at = (h * TILES + k) * H
                    last = pe.matmul(heads[slot][:, at:at + H], hidden[:, h, k * P:(k + 1) * P], a2_sb[:, :],
                                     start=True, stop=True)
                last.then_inc(s_heads, 1)

            def pair_step(q, slot, turn):
                for h in range(2):
                    g = 2 * q + h
                    if h == 0:
                        pe.wait_ge(s_edge[slot], 16 * (turn + 1))
                    wait(pe, s_hidden, g - 1)
                    product = pe.matmul(pre[h][:, :], w_fold[:, 2 + h, :], edge[:, slot, :], start=True, stop=False,
                                        skip_group_check=True)
                    if h == 1:
                        product.then_inc(s_edge_used, 1)
                    else:
                        word = word_of(pe, g)
                    first, more = window_of(word, h)
                    pe.wait_ge(s_onehot, g + 1)
                    for c in range(3):
                        pe.matmul(pre[h][:, :], flat[:, bass.ds(first * (3 * P) + c * P, P)], onehot[:, h, :],
                                  start=False, stop=False, skip_group_check=True)
                    with pe.If(more > 0):
                        n_extra, n_before = rounds_of(pe, g)
                        with pe.Fori(0, n_extra) as r:
                            pe.wait_ge(s_extra, n_before + r + 1)
                            done = (first + r * EXTRA).with_bounds(min_val=0, max_val=blocks - 1)
                            for w in range(EXTRA):
                                for c in range(3):
                                    at = done * (3 * P) + (1 + w) * 3 * P + c * P
                                    last = pe.matmul(pre[h][:, :], flat[:, bass.ds(at, P)], extra[:, w, :],
                                                     start=False, stop=False, skip_group_check=True)
                            last.then_inc(s_extra_used, 1)
                    pe.wait_ge(s_rows[2 * slot + h], 64 * (turn + 1))
                    for k in range(TILES):
                        last = pe.matmul(pre[h][:, k * P:(k + 1) * P], rows[:, 2 * slot + h, k, :], ident[:, :],
                                         start=False, stop=True, skip_group_check=True)
                    last.then_inc(s_pre, 1)
                    if h == 1:
                        pe.wait_ge(s_hidden, g)
                        wait(pe, s_head_b, q - 1)
                        score_mm(0, slot)
                    elif not isinstance(q, int) or q > 0:
                        pe.wait_ge(s_hidden, g)
                        score_mm(1, 1 - slot)

            def node_step(i, u):
                if u == 0 and valid(i):
                    if isinstance(i, int) and i == 0:
                        pe.wait_ge(s_late, 16 * NODE_WEIGHTS)
                    pe.wait_ge(s_node_x, 16 * (i + 1))
                    wait(pe, s_node_y, i)
                    pe.matmul(wide[0][:, 0:P], node_x[:, :], wn_sb[:, :], start=True, stop=True).then_inc(s_node_h, 1)

            over_pairs(pe, pairs, blocks, pair_step, node_step)
            pe.wait_ge(s_hidden, groups)
            score_mm(1, (pairs - 1) % 2)

            pe.wait_ge(s_exp, 2)
            pe.matmul(pre[0][:, 0:1], ones_f[:, :], cols[:, 13:14], start=True, stop=False)
            pe.matmul(pre[0][:, 0:1], ones_f[:, :], cols[:, 14:15], start=False, stop=True).then_inc(s_total, 1)
            pe.wait_ge(s_soft, 5)
            for c in range(key_cols):
                last = pe.matmul(pre[1][0:key_parts, c:c + 1], nonzero[:, c * key_parts:(c + 1) * key_parts],
                                 ones_b[:, :], start=True, stop=True)
            last.then_inc(s_counts, 1)

            pe.wait_ge(s_left, 1)
            left = pe.value_load(count_i[0:1, 0:1], min_val=1, max_val=tiles)
            with pe.Fori(0, left) as i:
                pe.wait_ge(s_seg_x, 16 * i + 16)
                pe.wait_ge(s_seg, 10 * i + 3)
                pe.matmul(pre[0][:, 0:P], seg_x[:, :], seg_w[:, :], start=True, stop=True).then_inc(s_seg_mm, 1)
                pe.wait_ge(s_seg, 10 * i + 4)
                pe.matmul(pre[0][:, P:2 * P], seg_t[:, :], wv_sb[:, :], start=True, stop=False)
                pe.matmul(pre[0][:, P:2 * P], seg_w[:, :], bv_row[:, :], start=False, stop=True).then_inc(s_seg_mm, 1)

        @block.vector
        def _(dve):
            dve.memset(we_in[:, 0, DE:P], 0.0).then_inc(s_cast, 1)
            dve.memset(we_in[:, 1, 0:DE], 0.0).then_inc(s_cast, 1)
            dve.wait_ge(s_iota, 2)
            dve.tensor_copy(iota_f[:, :], iota_i[:, :]).then_inc(s_cast, 1)
            dve.memset(cols[:, 12:13], EPS).then_inc(s_cast, 1)
            dve.wait_ge(s_const, MADE)
            dve.wait_ge(s_fold, 1)
            fold = heads[0][:, 0:4 * P].rearrange("p (c n) -> p c n", c=4)
            dve.tensor_copy(w_fold[:, 0:2, :], fold[:, 0:2, :]).then_inc(s_folded, 1)

            sv = span_in.rearrange("p (g n) -> p g n", g=info_cols)

            def table_step(c, slot, turn):
                dve.wait_ge(s_pk_hi, c + 1)
                dve.wait_ge(s_pq_stage, c + 1)
                wait(dve, s_pk_lo, c - WIDE + 1)
                both = wide[slot % WIDE][:, :].rearrange("p (j t d) -> p j t d", j=CHUNK, t=2)
                dve.tensor_tensor(pk_rest[:, slot % WIDE, :].rearrange("p (j d) -> p j d", j=CHUNK), both[:, :, 1, :],
                                  pk[:, bass.ds(c * CHUNK, CHUNK), 0, :], ALU.subtract).then_inc(s_pk_rest, 1)
                if isinstance(c, int) and c < info_cols:
                    if c == 0:
                        dve.wait_ge(s_span_in, 16)
                    for n, op in enumerate((ALU.min, ALU.max)):
                        dve.tensor_reduce(spans[:, n, c:c + 1], sv[:, c, :], AX_X, op).then_inc(s_span, 1)
                if isinstance(c, int) and c == span_peel - 1:
                    spans_done()
                if isinstance(c, int) and c >= chunks - len(INFO_STEPS):
                    INFO_STEPS[c - chunks + len(INFO_STEPS)]()

            def spans_done():
                dve.wait_ge(s_fold, 2)
                dve.tensor_copy(w_fold[:, 2:4, :], fold[:, 2:4, :]).then_inc(s_folded, 1)
                dve.tensor_tensor(bias_col[:, 0:1], heads[1][:, 0:1], bcols[:, 3:4], ALU.add).then_inc(s_folded, 1)
                at = 2 * info_cols
                dve.wait_ge(s_span, at)
                dve.tensor_scalar(spans[:, 2:4, :], spans[:, 0:2, :], 7, None, ALU.logical_shift_right).then_inc(
                    s_span, 1)
                dve.wait_ge(s_folded, 3)
                dve.tensor_scalar(bias_col[:, 1:2], bias_col[:, 0:1], SLOPE, None, ALU.mult).then_inc(s_bias_col, 1)
                dve.wait_ge(s_span, at + 1)
                dve.tensor_tensor(spans[:, 4, :], spans[:, 3, :], spans[:, 2, :], ALU.subtract).then_inc(s_span, 1)
                dve.wait_ge(s_span, at + 2)
                scale = (1 << 16) // EXTRA + (EXTRA > 1)
                dve.tensor_scalar(spans[:, 5, :], spans[:, 4, :], float(EXTRA - 1), float(scale), ALU.add,
                                  ALU.mult).then_inc(s_span, 1)
                dve.wait_ge(s_span, at + 3)
                both = spans[:, 6:8, :].rearrange("p a b -> p (a b)").rearrange("p (g c) -> p g c", c=2)
                dve.tensor_copy(both[:, :, 0], spans[:, 2, :]).then_inc(s_span, 1)
                dve.tensor_scalar(both[:, :, 1], spans[:, 5, :], 16, None, ALU.logical_shift_right).then_inc(s_span, 1)

            def rounds():
                dve.wait_ge(s_span_row, 16)
                dve.tensor_copy(rounds_f[:, :], span_row[:, :, 1]).then_inc(s_info, 1)
                dve.wait_ge(s_info, 1)
                dve.wait_ge(s_const, 5)
                dve.tensor_tensor_scan(sums_f[:, :], rounds_f[:, :], zeros_f[:, :], 0.0, ALU.add, ALU.add).then_inc(
                    s_info, 1)

            def rounds_before():
                dve.wait_ge(s_info, 2)
                dve.tensor_copy(info[:, :, 0:2], span_row[:, :, :]).then_inc(s_info, 1)
                dve.tensor_tensor(info[:, :, 2], sums_f[:, :], rounds_f[:, :], ALU.subtract).then_inc(s_info, 1)

            def words():
                dve.wait_ge(s_info, 4)
                dve.tensor_scalar(rounds_f[:, :], rounds_f[:, :], 1.0, float(MORE), ALU.min, ALU.mult).then_inc(
                    s_info, 1)
                dve.wait_ge(s_info, 5)
                dve.tensor_tensor(sums_f[:, :], rounds_f[:, :], info[:, :, 0], ALU.add).then_inc(s_info, 1)

            def double_words():
                dve.wait_ge(s_info, 6)
                dve.scalar_tensor_tensor(out=info[:, 0:groups - 1, 3], in0=sums_f[:, 1:groups], scalar=2.0 * MORE,
                                         in1=sums_f[:, 0:groups - 1], op0=ALU.mult, op1=ALU.add).then_inc(s_info, 1)
                dve.tensor_copy(info[:, groups - 1:groups, 3], sums_f[:, groups - 1:groups]).then_inc(s_info, 1)

            INFO_STEPS = rounds, rounds_before, words, double_words
            roll(dve, chunks, span_peel, XA, table_step, tail=XA)
            dve.memset(pk[:, blocks:blocks + EXTRA, :, :], 0.0).then_inc(s_cast, 1)
            if n_edges % P:
                dve.tensor_scalar(cols[:, 4:5], iota_f[:, 0:1], float(n_edges % P), -0.5, ALU.is_lt,
                                  ALU.add).then_inc(s_cast, 1)
                dve.wait_ge(s_cast, 6)
                dve.tensor_scalar(cols[:, 4:5], cols[:, 4:5], 3e38, None, ALU.mult).then_inc(s_cast, 1)
                dve.wait_ge(s_cast, 7)
                dve.tensor_scalar(cols[:, 4:5], cols[:, 4:5], 2.0, None, ALU.mult).then_inc(s_cast, 1)

            dve.wait_ge(s_info, 8)
            dve.wait_ge(s_weights, 16 * EDGE_WEIGHTS)

            def windows(q, slot, turn, h, word, part):
                    g = 2 * q + h
                    dst = dst_b[:, slot, h * GROUP:(h + 1) * GROUP]
                    first, more = window_of(word, part)
                    if h == 0:
                        dve.wait_ge(s_dst[slot], 16 * (turn + 1))
                    wait(dve, s_pre, g - 1)
                    dve.tensor_scalar(onehot[:, h, :], dst, iota_f[:, bass.ds(first, 1)], None,
                                      ALU.is_equal).then_inc(s_onehot, 1)
                    with dve.If(more > 0):
                        n_extra, n_before = rounds_of(dve, g)
                        with dve.Fori(0, n_extra) as r:
                            dve.wait_ge(s_extra_used, n_before + r + 1)
                            done = (first + r * EXTRA).with_bounds(min_val=0, max_val=blocks - 1)
                            for w in range(EXTRA):
                                last = dve.tensor_scalar(extra[:, w, :], dst,
                                                         iota_f[:, bass.ds(done + (1 + w), 1)], None,
                                                         ALU.is_equal)
                            last.then_inc(s_extra, 1)

            def relu(g, h):
                dve.wait_ge(s_sloped, g + 1)
                wait(dve, s_heads, g - 1)
                dve.scalar_tensor_tensor(out=hidden[:, h, :], in0=pre[h][:, :], scalar=bias_col[:, 0:1],
                                         in1=sloped[:, h, :], op0=ALU.add, op1=ALU.max).then_inc(s_hidden, 1)

            def scores(q, slot):
                dve.wait_ge(s_heads, 2 * q + 2)
                dve.tensor_tensor(head_b[:, :, :], heads[slot][:, 0:PT * H].rearrange("p (t h) -> p t h", h=H),
                                  b2_row[:, None, :].to_broadcast([P, PT, H]), ALU.add).then_inc(s_head_b, 1)
                dve.wait_ge(s_head_b, q + 1)
                dve.scalar_tensor_tensor(out=head_l[:, :, :], in0=head_b[:, :, :], scalar=SLOPE, in1=head_b[:, :, :],
                                         op0=ALU.mult, op1=ALU.max).then_inc(s_head_l, 1)
                dve.wait_ge(s_head_l, q + 1)
                dve.tensor_reduce(score[:, bass.ds(q * PT, PT)], head_l[:, :, :], AX_X, ALU.add).then_inc(s_score, 1)

            def pair_step(q, slot, turn):
                word = word_of(dve, 2 * q + 1)
                if not isinstance(q, int) or q > 0:
                    relu(2 * q - 1, 1)
                windows(q, slot, turn, 1, word, 0)
                relu(2 * q, 0)
                if not isinstance(q, int) or q < pairs - 1:
                    windows(q + 1, 1 - slot, turn + slot, 0, word, 1)
                if not isinstance(q, int) or q > 0:
                    scores(q - 1, 1 - slot)

            def moments(n, b, rows_of, waited):
                waited()
                dve.bn_stats(node_st[:, n, :], rows_of[:, :]).then_inc(s_node_st[n], 1)
                dve.wait_ge(s_node_st[n], b + 1)
                dve.sem_inc(s_passed, 1)
                dve.bn_aggr(node_m[:, n, 0:2], node_st[:, n, :]).then_inc(s_node_m[n], 1)

            def inverse(n, b):
                dve.wait_ge(s_node_sd[n], b + 1)
                dve.reciprocal(node_m[:, n, 3:4], node_m[:, n, 2:3]).then_inc(s_node_inv[n], 1)
                dve.wait_ge(s_node_inv[n], b + 1)

            def node_step(i, u):
                if u == 0 and valid(i - 1):
                    b = i - 1
                    inverse(0, b)
                    wait(dve, s_node_o, b)
                    dve.tensor_scalar(node_t[:, :], node_y[:, :], node_m[:, 0, 0:1], node_m[:, 0, 3:4], ALU.subtract,
                                      ALU.mult).then_inc(s_node_t, 1)
                    dve.wait_ge(s_node_t, 4 * b + 1)
                    dve.tensor_tensor(node_t[:, :], node_t[:, :], gamma_row[:, :], ALU.mult).then_inc(s_node_t, 1)
                    dve.wait_ge(s_node_t, 4 * b + 2)
                    dve.tensor_tensor(node_t[:, :], node_t[:, :], beta_row[:, :], ALU.add).then_inc(s_node_t, 1)
                    dve.wait_ge(s_node_t, 4 * b + 3)
                    dve.wait_ge(s_node_r, 16 * (b + 1))
                    dve.tensor_tensor(node_t[:, :], node_t[:, :], node_r[:, :], ALU.add).then_inc(s_node_t, 1)
                    moments(1, b, node_t, lambda: dve.wait_ge(s_node_t, 4 * b + 4))
                if u == 1 and valid(i - 1):
                    b = i - 1
                    inverse(1, b)
                    wait(dve, s_node_out, 16 * b)
                    dve.tensor_scalar(node_o[:, :], node_t[:, :], node_m[:, 1, 0:1], node_m[:, 1, 3:4], ALU.subtract,
                                      ALU.mult).then_inc(s_node_o, 1)
                if u == 1 and valid(i):
                    if isinstance(i, int) and i == 0:
                        dve.wait_ge(s_late, 16 * NODE_WEIGHTS)
                    dve.wait_ge(s_node_h, i + 1)
                    wait(dve, s_node_y_out, 16 * i)
                    dve.tensor_tensor(node_y[:, :], wide[0][:, 0:P], bn_row[:, :], ALU.add).then_inc(s_node_y, 1)
                    moments(0, i, node_y, lambda: dve.wait_ge(s_node_y, i + 1))

            windows(0, 0, 0, 0, word_of(dve, 0), 0)
            over_pairs(dve, pairs, blocks, pair_step, node_step)
            dve.wait_ge(s_score, pairs - 1)
            full = n_edges // P
            settled = min(full, (pairs - 1) * PT)
            dve.tensor_reduce(score[:, tiles:tiles + 1], score[:, 0:settled], AX_X, ALU.max).then_inc(s_max_part, 1)
            relu(groups - 1, 1)
            scores(pairs - 1, (pairs - 1) % 2)

            dve.wait_ge(s_score, pairs)
            if n_edges % P:
                dve.wait_ge(s_cast, 8)
                dve.tensor_tensor(score[:, full:full + 1], score[:, full:full + 1], cols[:, 4:5],
                                  ALU.min).then_inc(s_soft, 1)
            else:
                dve.memset(cols[:, 4:5], 0.0).then_inc(s_soft, 1)
            used = full + (n_edges % P > 0)
            if used < tiles:
                dve.memset(score[:, used:tiles], -3e38).then_inc(s_cast, 1)
                dve.wait_ge(s_cast, 9 if n_edges % P else 6)
            dve.wait_ge(s_soft, 1)
            dve.wait_ge(s_max_part, 1)
            dve.tensor_reduce(cols[:, 0:1], score[:, settled:tiles + 1], AX_X, ALU.max).then_inc(s_soft, 1)
            dve.wait_ge(s_max, 1)
            dve.tensor_scalar(cols[:, 2:3], cols[:, 1:2], -1.0 / H, None, ALU.mult).then_inc(s_soft, 1)
            for n, (a, b) in enumerate(halves):
                dve.wait_ge(s_exp, n + 1)
                dve.tensor_scalar(nonzero[:, a:b], score[:, a:b], 0.0, None, ALU.not_equal).then_inc(s_soft, 1)
            dve.wait_ge(s_total, 1)
            dve.reciprocal(cols[:, 5:6], pre[0][:, 0:1]).then_inc(s_soft, 1)
            dve.wait_ge(s_counts, 1)
            dve.wait_ge(s_const, 9)
            kp = key_parts
            dve.tensor_scalar(flag[0:kp, :], pre[1][0:kp, 0:key_cols], 0.0, None, ALU.is_gt).then_inc(s_counts, 1)
            dve.tensor_scalar(key[0:kp, :], row_i[0:kp, 0:key_cols], float(-kp), KEY, ALU.mult, ALU.add).then_inc(
                s_counts, 1)
            dve.wait_ge(s_counts, 3)
            dve.tensor_reduce(cols[:, 6:7], flag[:, :], AX_X, ALU.add).then_inc(s_counts, 1)
            dve.tensor_scalar(key[0:kp, :], key[0:kp, :], iota_f[0:kp, 0:1], None, ALU.subtract).then_inc(s_seg_key, 1)
            dve.wait_ge(s_seg_key, 1)
            dve.tensor_tensor(key[:, :], key[:, :], flag[:, :], ALU.mult).then_inc(s_seg_key, 1)
            dve.wait_ge(s_counts, 5)
            dve.tensor_copy(count_i[:, :], cols[0:1, 7:8]).then_inc(s_left, 1)
            dve.wait_ge(s_left, 1)
            dve.wait_ge(s_seg_key, 2)
            left = dve.value_load(count_i[0:1, 0:1], min_val=1, max_val=tiles)

            with dve.Fori(0, left) as i:
                dve.tensor_reduce(cols[:, 8:9], key[:, :], AX_X, ALU.max).then_inc(s_seg_key, 1)
                dve.wait_ge(s_seg_max, i + 1)
                dve.tensor_scalar(tile_i[:, :], cols[0:1, 9:10], -1.0, KEY, ALU.mult, ALU.add).then_inc(s_seg_tile, 1)
                dve.scalar_tensor_tensor(out=key[:, :], in0=key[:, :], scalar=cols[:, 9:10], in1=key[:, :],
                                         op0=ALU.not_equal, op1=ALU.mult).then_inc(s_seg_key, 1)
                dve.wait_ge(s_seg_tile, i + 1)
                dve.sem_inc(s_passed, 1)
                t = dve.value_load(tile_i[0:1, 0:1], min_val=0, max_val=tiles - 1)
                dve.tensor_scalar(seg_f[:, 0:1], score[:, bass.ds(t, 1)], cols[:, 5:6], None, ALU.mult).then_inc(
                    s_seg, 1)
                dve.wait_ge(s_seg_src, 16 * i + 16)
                dve.tensor_copy(seg_f[:, 1:2], seg_col[:, 0:1]).then_inc(s_seg, 1)
                dve.wait_ge(s_seg, 10 * i + 2)
                dve.wait_ge(s_seg_row, 16 * i + 16)
                dve.tensor_scalar(seg_w[:, :], seg_row[:, :], seg_f[:, 1:2], seg_f[:, 0:1], ALU.is_equal,
                                  ALU.mult).then_inc(s_seg, 1)
                dve.wait_ge(s_seg_mm, 2 * i + 1)
                dve.tensor_copy(seg_t[:, :], pre[0][:, 0:P]).then_inc(s_seg, 1)
                dve.scalar_tensor_tensor(out=seg_s[:, :], in0=seg_row[:, :], scalar=seg_f[:, 1:2], in1=before[:, :],
                                         op0=ALU.is_equal, op1=ALU.mult).then_inc(s_seg, 1)
                dve.wait_ge(s_seg, 10 * i + 5)
                dve.tensor_reduce(seg_f[:, 2:3], seg_s[:, :], AX_X, ALU.max).then_inc(s_seg, 1)
                dve.tensor_tensor(seg_f[:, 3:4], iota_f[:, 0:1], seg_f[:, 1:2], ALU.subtract).then_inc(s_seg, 1)
                dve.wait_ge(s_seg, 10 * i + 7)
                dve.tensor_scalar(seg_f[:, 4:5], seg_f[:, 3:4], float(n_pad), seg_f[:, 2:3], ALU.add,
                                  ALU.mult).then_inc(s_seg, 1)
                dve.wait_ge(s_seg, 10 * i + 8)
                dve.tensor_tensor(seg_to[:, :], seg_f[:, 4:5], seg_f[:, 1:2], ALU.add).then_inc(s_seg, 1)
                dve.wait_ge(s_seg_mm, 2 * i + 2)
                dve.wait_ge(s_seg_y, 16 * i + 16)
                dve.tensor_tensor(seg_y[:, :], seg_y[:, :], pre[0][:, P:2 * P], ALU.add).then_inc(s_seg, 1)
                dve.wait_ge(s_seg, 10 * i + 10)
                for n, v in enumerate((seg_y, seg_x)):
                    at = 11 * i + 7 * n
                    dve.bn_stats(seg_st[:, n, :], v[:, :]).then_inc(s_seg_ln, 1)
                    dve.wait_ge(s_seg_ln, at + 1)
                    dve.sem_inc(s_passed, 1)
                    dve.bn_aggr(seg_m[:, n, 0:2], seg_st[:, n, :]).then_inc(s_seg_ln, 1)
                    dve.wait_ge(s_seg_sd, 2 * i + n + 1)
                    dve.reciprocal(seg_m[:, n, 3:4], seg_m[:, n, 2:3]).then_inc(s_seg_ln, 1)
                    dve.wait_ge(s_seg_ln, at + 3)
                    dve.tensor_scalar((seg_x if n == 0 else seg_o)[:, :], v[:, :], seg_m[:, n, 0:1], seg_m[:, n, 3:4],
                                      ALU.subtract, ALU.mult).then_inc(s_seg_ln, 1)
                    if n == 0:
                        dve.wait_ge(s_seg_ln, at + 4)
                        dve.tensor_tensor(seg_x[:, :], seg_x[:, :], gamma_row[:, :], ALU.mult).then_inc(s_seg_ln, 1)
                        dve.wait_ge(s_seg_ln, at + 5)
                        dve.tensor_tensor(seg_x[:, :], seg_x[:, :], beta_row[:, :], ALU.add).then_inc(s_seg_ln, 1)
                        dve.wait_ge(s_seg_ln, at + 6)
                        dve.wait_ge(s_seg_xs, 16 * i + 16)
                        dve.tensor_tensor(seg_x[:, :], seg_x[:, :], seg_xs[:, :], ALU.add).then_inc(s_seg_ln, 1)
                        dve.wait_ge(s_seg_ln, at + 7)
                dve.wait_ge(s_seg_y_out, 16 * i + 16)
                dve.wait_ge(s_seg_out, 16 * i + 16)


_ROWS = ("x_rows", "x_blocks", "edges", "src_pairs", "dst_pairs", "src_tiles", "dst_tiles", "wqT", "wkT",
         "weT", "wv", "wn", "bn", "bq", "bk", "bv", "be", "A1", "b1", "A2", "b2", "gamma", "beta")


def lay_out(x, src, dst, edge_attr_64, **w):
    x, src, dst, edge_attr = (np.asarray(a) for a in (x, src, dst, edge_attr_64))
    w = {k.replace("L0_gnn_", ""): np.asarray(v) for k, v in w.items()}
    n, d = x.shape
    e, de = edge_attr.shape
    step = P * CHUNK
    chunks = -(-n // step)
    pairs = -(-e // PAIR)
    pairs += 1 - pairs % 2
    xp = np.pad(x, ((0, chunks * step - n), (0, 0)))
    ep = np.pad(edge_attr, ((0, pairs * PAIR - e), (0, 0)))
    sp, dp = (np.pad(a, (0, pairs * PAIR - e), mode="edge") for a in (src, dst))
    arrays = {
        "x_rows": xp,
        "x_blocks": xp.reshape(chunks * CHUNK, P, d).transpose(0, 2, 1),
        "edges": ep.reshape(pairs, 2, GROUP, de).transpose(0, 1, 3, 2).reshape(pairs, 2 * de, GROUP),
        "src_pairs": sp.reshape(pairs, PT, P).transpose(0, 2, 1),
        "dst_pairs": dp.reshape(pairs, PAIR),
        "src_tiles": sp.reshape(pairs * PT, P),
        "dst_tiles": dp.reshape(pairs * PT, P),
        "wqT": w["Wq"].T, "wkT": w["Wk"].T, "weT": w["We"].T, "wv": w["Wv"], "wn": w["Wn"],
        "bn": w["bn"], "bq": w["bq"], "bk": w["bk"], "bv": w["bv"], "be": w["be"], "A1": w["A1"], "b1": w["b1"],
        "A2": w["A2"], "b2": w["b2"], "gamma": w["gamma"], "beta": w["beta"],
    }
    return {k: np.ascontiguousarray(arrays[k]) for k in _ROWS}


def kernel(**inputs):
    import concourse.bacc as bacc
    from concourse.bass_utils import run_bass_kernel_spmd

    n, d = inputs["x"].shape
    arrays = {f"in_{k}_dram": a for k, a in lay_out(**inputs).items()}
    nc = bacc.Bacc("TRN2", target_bir_lowering=False, num_devices=1)
    args = [nc.dram_tensor(k, a.shape, mybir.dt.from_np(a.dtype), kind="ExternalInput").ap() for k, a in arrays.items()]
    out = nc.dram_tensor("out_0_dram", (arrays["in_x_rows_dram"].shape[0] + OUT_MORE, d), F32, kind="ExternalOutput").ap()
    build(nc, *args, out, inputs["edge_attr_64"].shape[0])
    r = run_bass_kernel_spmd(nc, [arrays], core_ids=[0])
    return r.results[0]["out_0_dram"][:n]
```
